# Optimizing a Trainium2 kernel written in Bass

```python
import numpy as np
import jax
import jax.numpy as jnp

def _softmax(x, axis=-1):
    return jax.nn.softmax(x, axis=axis)

def _gelu(x):
    return jax.nn.gelu(x, approximate=True)

def _silu(x):
    return jax.nn.silu(x)

def _sigmoid(x):
    return jax.nn.sigmoid(x)

def _layernorm(x, axis=-1, eps=1e-05):
    m = jnp.mean(x, axis=axis, keepdims=True)
    v = jnp.var(x, axis=axis, keepdims=True)
    return (x - m) / jnp.sqrt(v + eps)

def _scatter_add(tgt, idx, src, axis=0):
    return tgt.at[idx].add(src)

def _segment_sum(src, seg, n):
    return jax.ops.segment_sum(src, seg, n)
kernel_name = 'mk_conv_preact_d4_conv_nchw1024_r4_d56de8'

def setup_inputs(seed: int=0):
    np.random.seed(seed)
    _w = jnp.asarray

    def _rec_inputs():
        import jax
        import jax.numpy as jnp
        _gk = jax.random.key(seed)
        x = -0.000125 + 0.9999 * jax.random.normal(jax.random.fold_in(_gk, 1), (8, 256, 16, 16), jnp.float32)
        return x
    x = _rec_inputs()

    def _L0_conv_setup():
        import jax, jax.numpy as jnp
        import numpy as np
        K = 5
        PAD = K // 2
        EPS = 1e-12
        key = jax.random.key(seed)
        k1, k2, k3 = jax.random.split(key, 3)
        b, c, h, w = (8, 256, 16, 16)
        out_ch = 256
        feature = jax.random.normal(k1, (b, c, h, w), dtype=jnp.float32)
        conv_w = jax.random.normal(k2, (out_ch, c + K * K), dtype=jnp.float32) * 0.02
        conv_b = jax.random.normal(k3, (out_ch,), dtype=jnp.float32) * 0.02
        return {'feature': feature, 'conv_w': conv_w, 'conv_b': conv_b}
    _L0_conv_all = _L0_conv_setup()
    _L0_conv_in = {k: v for k, v in _L0_conv_all.items() if k in ('conv_w', 'conv_b')}
    del _L0_conv_all

    def _L1_conv_setup():
        import jax, jax.numpy as jnp
        import numpy as np
        R = 32
        key = jax.random.key(seed)
        k1, k2, k3 = jax.random.split(key, 3)
        B, C, H, W = (4, 256, 32, 32)
        d = C // R
        x = jax.random.normal(k1, (B, C, H, W), dtype=jnp.float32)
        w_qkv = jax.random.normal(k2, (3 * d, d), dtype=jnp.float32) * 0.1
        b_qkv = jax.random.normal(k3, (3 * d,), dtype=jnp.float32) * 0.01
        return {'x': x, 'w_qkv': w_qkv, 'b_qkv': b_qkv}
    _L1_conv_all = _L1_conv_setup()
    _L1_conv_in = {k: v for k, v in _L1_conv_all.items() if k in ('w_qkv', 'b_qkv')}
    del _L1_conv_all

    def _L2_conv_setup():
        import jax, jax.numpy as jnp
        import numpy as np
        B, C, H, Wd = (16, 256, 16, 16)
        key = jax.random.key(seed)
        k1, k2, k3 = jax.random.split(key, 3)
        x = jax.random.normal(k1, (B, C, H, Wd), dtype=jnp.float32)
        W = jax.random.normal(k2, (C, C), dtype=jnp.float32) / jnp.sqrt(jnp.float32(C))
        gamma = jax.random.normal(k3, (1,), dtype=jnp.float32)
        return {'x': x, 'W': W, 'gamma': gamma}
    _L2_conv_all = _L2_conv_setup()
    _L2_conv_in = {k: v for k, v in _L2_conv_all.items() if k in ('W', 'gamma')}
    del _L2_conv_all

    def _L3_conv_setup():
        import jax, jax.numpy as jnp
        import numpy as np
        B, C, H, W = (2, 256, 16, 16)
        E, TOP_K = (8, 2)
        FFN = C
        key = jax.random.key(seed)
        ks = jax.random.split(key, 5)
        s = 0.02
        return {'hidden_states': jax.random.normal(ks[0], (B, C, H, W), jnp.float32), 'gate_w': jax.random.normal(ks[1], (E, C), jnp.float32) * s, 'w1': jax.random.normal(ks[2], (E, FFN, C), jnp.float32) * s, 'w2': jax.random.normal(ks[3], (E, C, FFN), jnp.float32) * s, 'w3': jax.random.normal(ks[4], (E, FFN, C), jnp.float32) * s}
    _L3_conv_all = _L3_conv_setup()
    _L3_conv_in = {k: v for k, v in _L3_conv_all.items() if k in ('gate_w', 'w1', 'w2', 'w3')}
    del _L3_conv_all
    return {'x': x, 'L0_conv_conv_w': _L0_conv_in['conv_w'], 'L0_conv_conv_b': _L0_conv_in['conv_b'], 'L1_conv_w_qkv': _L1_conv_in['w_qkv'], 'L1_conv_b_qkv': _L1_conv_in['b_qkv'], 'L2_conv_W': _L2_conv_in['W'], 'L2_conv_gamma': _L2_conv_in['gamma'], 'L3_conv_gate_w': _L3_conv_in['gate_w'], 'L3_conv_w1': _L3_conv_in['w1'], 'L3_conv_w2': _L3_conv_in['w2'], 'L3_conv_w3': _L3_conv_in['w3']}

def reference(x, L0_conv_conv_w, L0_conv_conv_b, L1_conv_w_qkv, L1_conv_b_qkv, L2_conv_W, L2_conv_gamma, L3_conv_gate_w, L3_conv_w1, L3_conv_w2, L3_conv_w3):
    import jax
    import jax.numpy as jnp

    def _L0_conv_ref(feature, conv_w, conv_b):
        import jax, jax.numpy as jnp
        import numpy as np
        K = 5
        PAD = K // 2
        EPS = 1e-12
        b, c, h, w = feature.shape
        norm = jnp.sqrt(jnp.sum(feature * feature, axis=1, keepdims=True))
        fn = feature / jnp.maximum(norm, EPS)
        fp = jnp.pad(fn, ((0, 0), (0, 0), (PAD, PAD), (PAD, PAD)))
        corr = jnp.stack([jnp.sum(fp[:, :, r:h + r, cc:w + cc] * fn, axis=1) for cc in range(K) for r in range(K)], axis=1)
        cat = jnp.concatenate([feature, corr], axis=1)
        y = jnp.einsum('oc,bchw->bohw', conv_w, cat) + conv_b[None, :, None, None]
        return jax.nn.relu(y)

    def _L1_conv_ref(x, w_qkv, b_qkv):
        import jax, jax.numpy as jnp
        import numpy as np
        R = 32
        B, C, H, W = x.shape
        d = C // R
        HW = H * W
        xr = x.reshape(B, C, HW).transpose(0, 2, 1).reshape(B, HW, R, d).transpose(0, 2, 1, 3)
        qkv = jnp.einsum('brnd,ed->brne', xr, w_qkv) + b_qkv
        q, k, v = jnp.split(qkv, 3, axis=-1)
        attn = jnp.einsum('brnd,brmd->brnm', q, k)
        attn = jax.nn.softmax(attn, axis=0)
        out = jnp.einsum('brnm,brmd->brnd', attn, v)
        out = out.transpose(0, 2, 1, 3).reshape(B, HW, C).reshape(B, -1, H, W)
        return out

    def _L2_conv_ref(x, W, gamma):
        import jax, jax.numpy as jnp
        import numpy as np
        B, C, H, Wd = (16, 256, 16, 16)
        b, c, h, w = x.shape
        xf = x.reshape(b, c, h * w)
        convx = jnp.einsum('oc,bcn->bon', W, xf)
        xxT = jnp.einsum('bcn,bdn->bcd', xf, xf)
        o = jnp.einsum('bcd,bdn->bcn', xxT, convx)
        o = gamma[0] * o + xf
        return o.reshape(b, c, h, w)

    def _L3_conv_ref(hidden_states, gate_w, w1, w2, w3):
        import jax, jax.numpy as jnp
        import numpy as np
        B, C, H, W = (2, 256, 16, 16)
        E, TOP_K = (8, 2)
        FFN = C
        b, c = (hidden_states.shape[0], hidden_states.shape[1])
        space = hidden_states.shape[2:]
        x = jnp.transpose(hidden_states, (0, 2, 3, 1)).reshape(-1, c)
        logits = x @ gate_w.T
        probs = jax.nn.softmax(logits.astype(jnp.float32), axis=-1)
        rw, sel = jax.lax.top_k(probs, TOP_K)
        rw = rw / jnp.sum(rw, axis=-1, keepdims=True)
        rw = rw.astype(x.dtype)
        combine = jnp.sum(jax.nn.one_hot(sel, E, dtype=x.dtype) * rw[..., None], axis=1)
        out = jnp.zeros_like(x)
        for e in range(E):
            h = jax.nn.gelu(x @ w1[e].T, approximate=False) * (x @ w3[e].T)
            out = out + combine[:, e:e + 1] * (h @ w2[e].T)
        out = out.reshape(b, *space, c)
        return jnp.transpose(out, (0, 3, 1, 2))

    def _gn(v, G=32, eps=1e-05):
        B_, C_, H_, W_ = v.shape
        g = v.reshape(B_, G, C_ // G, H_, W_)
        m = jnp.mean(g, axis=(2, 3, 4), keepdims=True)
        s = jnp.var(g, axis=(2, 3, 4), keepdims=True)
        return ((g - m) / jnp.sqrt(s + eps)).reshape(v.shape)

    def _ln_c(v, eps=1e-06):
        m = jnp.mean(v, axis=1, keepdims=True)
        s = jnp.var(v, axis=1, keepdims=True)
        return (v - m) / jnp.sqrt(s + eps)

    def _ln_t(v, eps=1e-05):
        m = jnp.mean(v, axis=-1, keepdims=True)
        s = jnp.var(v, axis=-1, keepdims=True)
        return (v - m) / jnp.sqrt(s + eps)

    def _to_tokens(v):
        B_, C_, H_, W_ = v.shape
        return v.reshape(B_, C_, H_ * W_).transpose(0, 2, 1)

    def _from_tokens(t, like):
        B_, C_, H_, W_ = like.shape
        return t.transpose(0, 2, 1).reshape(B_, C_, H_, W_)
    x = x + _L0_conv_ref(_gn(x), L0_conv_conv_w, L0_conv_conv_b)
    x = x + _L1_conv_ref(_gn(x), L1_conv_w_qkv, L1_conv_b_qkv)
    x = x + _L2_conv_ref(_gn(x), L2_conv_W, L2_conv_gamma)
    x = x + _L3_conv_ref(_gn(x), L3_conv_gate_w, L3_conv_w1, L3_conv_w2, L3_conv_w3)
    return x

_drawn_inputs = setup_inputs


def setup_inputs(seed=0):
    import zlib

    import numpy as np

    out = dict(_drawn_inputs(seed))
    spreads = {}
    factors = {'L3_conv_gate_w': 25.024, 'L3_conv_w1': 33.827, 'L3_conv_w2': 24.804, 'L3_conv_w3': 26.235}
    for name, (base, spread) in spreads.items():
        noise = np.random.default_rng([zlib.crc32(name.encode()), seed]).standard_normal(out[name].shape)
        drawn = base * np.exp(spread * noise) if base else spread * noise
        out[name] = jnp.asarray(drawn.astype(out[name].dtype))
    for name, factor in factors.items():
        out[name] = (out[name] * factor).astype(out[name].dtype)
    return out
```

```python
import concourse.bass as bass
from concourse import mybir
from contextlib import ExitStack


def conv_stack_kernel(nc, x, conv_wT, conv_cT, conv_b, qkv_blocks, qk_bias, v_bias, gram_wT, gamma,
                      gate_wT, w13T, w2T, identity, ones, group_ones, edge_mask, expert_rank,
                      out):
    fp32, bf16 = mybir.dt.float32, mybir.dt.bfloat16
    ALU, ACT, AX = mybir.AluOpType, mybir.ActivationFunctionType, mybir.AxisListType.X

    B, C, SIDE = x.shape[0], x.shape[1], x.shape[2]
    N = SIDE * SIDE
    P = 128
    H = C // P
    T = B * N
    TILES = T // P
    CH = 512
    NCH = T // CH
    BPC = CH // N
    GROUP = 8
    K = 5
    NK = K * K
    REACH = (K // 2) * (SIDE + 1)
    WIN = 2 * REACH + 1
    ROW = P + 2 * REACH
    HEADS, D = 32, C // 32
    PARTS = 3
    KR = PARTS * PARTS * D
    HPG = 4
    NG = HEADS // HPG
    UPG = HPG * 4
    UNITS = NG * UPG
    UW = B * P
    ER = 8
    LAG = 4
    E = gate_wT.shape[1]
    EPS = 1e-5
    EPS_NORM2 = 1e-24

    gram_dram = nc.dram_tensor("gram_rows", (TILES, P, ROW), fp32, kind="Internal").ap()
    part_dram = nc.dram_tensor("qk_parts", (2, PARTS, C, T), bf16, kind="Internal").ap()

    ctx = ExitStack()
    with ctx:
        def sb(name, shape, dt=fp32):
            return ctx.enter_context(nc.sbuf_tensor(name, shape, dt))

        def sem(name):
            return ctx.enter_context(nc.semaphore(name))

        def view(t, off, dims, rows=P):
            width = 1
            for s in t.shape[1:]:
                width *= s
            return bass.AP(t, off, [[width, rows]] + [list(d) for d in dims])

        x_res = sb("x_res", [P, H, T])
        x_hat = sb("x_hat", [P, H, T])
        work = sb("work", [P, H * T])
        e_ring = sb("e_ring", [P, ER, UW])
        scratch = sb("scratch", [P, 6144])
        q_stack = sb("q_stack", [KR, HPG, T], bf16)
        k_stack = sb("k_stack", [KR, HPG, T], bf16)
        v_slot = sb("v_slot", [P, B * H, HPG, HPG * D])
        w13_sb = sb("w13_sb", [P, H, E * 2 * C])
        w2_sb = sb("w2_sb", [P, H, E * C])
        conv_wT_sb = sb("conv_wT_sb", [P, H, C])
        conv_cT_sb = sb("conv_cT_sb", [NK, C])
        conv_b_sb = sb("conv_b_sb", [P, H])
        qkv_sb = sb("qkv_sb", [P, 3, P])
        qk_bias_sb = sb("qk_bias_sb", [P, 2])
        v_bias_sb = sb("v_bias_sb", [P, D])
        gram_wT_sb = sb("gram_wT_sb", [P, H, C])
        gamma_sb = sb("gamma_sb", [P, 1])
        gate_sb = sb("gate_sb", [P, H, E])
        ident = sb("ident", [P, P])
        ident_neg = sb("ident_neg", [P, P], bf16)
        ones_sb = sb("ones_sb", [P, P])
        group_sb = sb("group_sb", [P, P])
        mask_sb = sb("mask_sb", [P, K])
        rank_sb = sb("rank_sb", [P, E])
        stats = sb("stats", [P, H * B, 6])
        sums = sb("sums", [P, H * B, 2])
        gn = sb("gn", [P, 8, H * B])
        m_bf = sb("m_bf", [P, 2, P], bf16)
        s_sum = sb("s_sum", [P, 2, P])
        s_ln = sb("s_ln", [P, 2, P])
        s_inv = sb("s_inv", [P, 2, P])
        o_sb = sb("o_sb", [P, CH])
        ps = ctx.enter_context(nc.psum_tensor("ps", [P, 8, CH], fp32))

        TPC = CH // P
        rnorm = scratch[:, 0:CH]
        GST = CH
        BAND = GST + 2 * TPC * ROW
        COR = BAND + TILES * WIN
        YB = COR + TILES * NK
        cor_t = view(e_ring, 0, [[1, T]], rows=NK)
        parts = scratch[:, :].bitcast(bf16).rearrange("p (s a t) -> p s a t", s=2, a=PARTS)
        rest = e_ring[:, 2:3, :].rearrange("p a (s c) -> p (a s) c", s=2)
        xt = e_ring[:, 0, :].rearrange("p (s n c) -> p s n c", s=2, n=2)
        xxt = e_ring[:, 1, :].rearrange("p (s n c) -> p s n c", s=2, n=2)
        cx = e_ring[:, 2, :].rearrange("p (s n c) -> p s n c", s=2, n=2)
        gelu1 = e_ring[:, 4, 0:CH].rearrange("p (s c) -> p s c", s=2)
        gated = e_ring[:, 5, 0:CH].rearrange("p (s c) -> p s c", s=2)
        gated_t = e_ring[:, 6, 0:CH].rearrange("p (s c) -> p s c", s=2)
        route = scratch[:, 0:7 * TILES * E].rearrange("p (i x) -> p i x", i=7)
        COL = 9 * TILES * E
        comb = scratch[:, 2048:2048 + E * TILES]
        y_acc = work[:, :].rearrange("p (t c) -> p t c", t=TILES)
        v_all = work[:, :].rearrange("p (t c) -> p t c", t=TILES)

        def bank(i):
            return ps[:, i, :]

        x_in = [sem(f"x_in{c}") for c in range(NCH)]
        consts_in, w_in = sem("consts_in"), sem("w_in")
        pool_init = sem("pool_init")
        gn_sums, gn_group, gn_var, gn_rstd, gn_coef = (sem("gn_" + n) for n in ("sums", "group", "var", "rstd", "coef"))
        xhat_act, xhat_dve = sem("xhat_act"), sem("xhat_dve")
        dve_chain, act_chain = sem("dve_chain"), sem("act_chain")
        sq_done, n2_done, n2_floor, rn_done, fn_done = (sem(n) for n in ("sq_done", "n2_done", "n2_floor", "rn_done", "fn_done"))
        gram_done, gram_row = sem("gram_done"), sem("gram_row")
        gram_out = [sem(f"gram_out{c}") for c in range(NCH)]
        band_in = [sem(f"band_in{c}") for c in range(NCH)]
        parts_out = [sem(f"parts_out{n}") for n in range(2 * H)]
        cor_done, cor_tr, cor_t_done, y_done, relu_done, x1_done = (
            sem(n) for n in ("cor_done", "cor_tr", "cor_t_done", "y_done", "relu_done", "x1_done"))
        qk_done, part1, rest_done, part2, part3 = (
            sem(n) for n in ("qk_done", "part1", "rest_done", "part2", "part3"))
        v_done, v_stored = sem("v_done"), sem("v_stored")
        stack_in = [sem(f"stack_in{i}") for i in range(HPG)]
        scores_done, max_done, sub_done, exp_done, sum_done, ln_done, r_done, norm_done, pv_done = (
            sem(n) for n in ("scores_done", "max_done", "sub_done", "exp_done", "sum_done", "ln_done", "r_done",
                             "norm_done", "pv_done"))
        acc_out, v_slot_ready, acc_tr, x2_added = (sem(n) for n in ("acc_out", "v_slot_ready", "acc_tr", "x2_added"))
        tr2_done, xt_done, cx_done, cx_out, xx_done, xx_out, o_done, x3_done, xsum_done = (
            sem(n) for n in ("tr2_done", "xt_done", "cx_done", "cx_out", "xx_done", "xx_out", "o_done", "x3_done",
                             "xsum_done"))
        logits_done, shifted, gate_exp, comb_done = (sem(n) for n in ("logits_done", "shifted", "gate_exp", "comb_done"))
        h_done, gelu_done, gated_done, gtr_done, gt_done, ye_done, ye_added = (
            sem(n) for n in ("h_done", "gelu_done", "gated_done", "gtr_done", "gt_done", "ye_done", "ye_added"))
        ytr_done, x4_done, out_done = sem("ytr_done"), sem("x4_done"), sem("out_done")

        block = ctx.enter_context(nc.Block())
        N_CONST = 14

        @block.sync
        def _(sp):
            for c in range(NCH):
                for h in range(H):
                    sp.dma_start(x_res[:, h, c * CH:(c + 1) * CH].rearrange("p (b n) -> p b n", b=BPC),
                                 x[c * BPC:(c + 1) * BPC, h * P:(h + 1) * P].rearrange("b p y x -> p b (y x)")
                                 ).then_inc(x_in[c], 16)
            for c in range(NCH + 1):
                if c < NCH:
                    sp.wait_ge(gram_row, TPC * (c + 1))
                    sp.dma_start(gram_dram[c * TPC:(c + 1) * TPC].rearrange("t p r -> p t r"),
                                 view(scratch, GST + (c % 2) * TPC * ROW, [[ROW, TPC], [1, ROW]])
                                 ).then_inc(gram_out[c], 16)
                if c >= 1:
                    sp.wait_ge(gram_out[c - 1], 16)
                    skew = bass.AP(gram_dram.tensor, (c - 1) * TPC * P * ROW, [[ROW + 1, P], [P * ROW, TPC], [1, WIN]])
                    sp.dma_start(view(scratch, BAND + (c - 1) * TPC * WIN, [[WIN, TPC], [1, WIN]]), skew
                                 ).then_inc(band_in[c - 1], 16)
            for n in range(2 * H):
                sp.wait_ge(part3, NCH * (n + 1))
                h, s = n // 2, n % 2
                dst = bass.AP(part_dram.tensor, (s * PARTS * C + h * P) * T, [[T, P], [C * T, PARTS], [1, T]])
                sp.dma_start(dst, parts[:, n % 2]).then_inc(parts_out[n], 16)

            def load_stack(g, i):
                row = (g * HPG + i) * D * T
                for a in range(PARTS):
                    rows = slice(a * PARTS * D, (a + 1) * PARTS * D)
                    q_src = bass.AP(part_dram.tensor, row, [[C * T, PARTS], [T, D], [1, T]])
                    k_src = bass.AP(part_dram.tensor, row + (PARTS + a) * C * T, [[0, PARTS], [T, D], [1, T]])
                    sp.dma_start(q_stack[rows, i, :], q_src).then_inc(stack_in[i], 16)
                    sp.dma_start(k_stack[rows, i, :], k_src).then_inc(stack_in[i], 16)

            for n in range(2 * H):
                sp.wait_ge(parts_out[n], 16)
            for i in range(HPG):
                load_stack(0, i)
            for h in range(H):
                sp.dma_start(w13_sb[:, h, :], w13T[h]).then_inc(w_in, 16)
                sp.dma_start(w2_sb[:, h, :], w2T[h]).then_inc(w_in, 16)
            with sp.Fori(0, NG - 1) as g:
                for i in range(HPG):
                    sp.wait_ge(scores_done, g * UPG + 4 * (i + 1))
                    load_stack(g + 1, i)
            for b in range(B):
                sp.wait_ge(x4_done, b + 1)
                sp.dma_start(out[b].rearrange("(h p) y x -> p h (y x)", p=P),
                             x_res[:, :, b * N:(b + 1) * N]).then_inc(out_done, 16)
            sp.wait_ge(out_done, 16 * B)

        @block.gpsimd
        def _(pool):
            nc.gpsimd.memset(view(scratch, GST, [[1, 2 * TPC * ROW]]), 0.0).then_inc(pool_init, 1)
            nc.gpsimd.memset(v_slot[:], 0.0).then_inc(pool_init, 1)
            pool.wait_ge(pool_init, 2)
            for n in range(2 * H * NCH):
                s, c = n // NCH, n % NCH
                pool.wait_ge(part2, n + 1)
                nc.gpsimd.tensor_tensor(parts[:, s % 2, 2, c * CH:(c + 1) * CH], rest[:, n % 2],
                                        parts[:, s % 2, 1, c * CH:(c + 1) * CH], ALU.subtract).then_inc(part3, 1)
            with pool.Fori(0, NG) as g:
                for u in range(UPG):
                    pool.wait_ge(r_done, g * UPG + u + 1)
                    ev = e_ring[:, u % ER, :].rearrange("p (b n) -> p b n", b=B)
                    nc.gpsimd.tensor_tensor(ev, ev, view(s_inv, (u % 2) * P, [[0, B], [1, P]]),
                                            ALU.mult).then_inc(norm_done, 1)
            for b in range(B):
                pool.wait_ge(xhat_act, B * 2 + b + 1)
                pool.wait_ge(xhat_dve, B * 2 + b + 1)
                nc.gpsimd.tensor_tensor(x_res[:, :, b * N:(b + 1) * N], x_res[:, :, b * N:(b + 1) * N],
                                        x_hat[:, :, b * N:(b + 1) * N], ALU.add).then_inc(xsum_done, 1)
            nc.gpsimd.memset(work[:], 0.0).then_inc(pool_init, 1)

        @block.scalar
        def _(act):
            chain = [0]

            def link(ins):
                chain[0] += 1
                ins.then_inc(act_chain, 1)
                act.wait_ge(act_chain, chain[0])

            for dst, src in ((group_sb[:], group_ones), (conv_wT_sb[:], conv_wT.rearrange("h p o -> p h o")),
                             (conv_cT_sb[:], conv_cT), (conv_b_sb[:], conv_b), (ones_sb[:], ones),
                             (ident[:], identity), (mask_sb[:], edge_mask),
                             (qkv_sb[:], qkv_blocks.rearrange("s p o -> p s o")), (qk_bias_sb[:], qk_bias),
                             (v_bias_sb[:], v_bias),
                             (gram_wT_sb[:], gram_wT.rearrange("h p o -> p h o")), (gamma_sb[:], gamma),
                             (gate_sb[:], gate_wT.rearrange("(h p) e -> p h e", p=P)), (rank_sb[:], expert_rank)):
                act.dma_start(dst, src).then_inc(consts_in, 16)

            def power(dst, src, done):
                link(nc.scalar.activation(dst, src, ACT.Ln))
                nc.scalar.activation(dst, dst, ACT.Exp, scale=-0.5).then_inc(done, 1)

            def normalise(k):
                act.wait_ge(gn_var, k + 1)
                power(gn[:, 3], gn[:, 2], gn_rstd)
                act.wait_ge(gn_coef, k + 1)
                for b in range(B):
                    nc.scalar.activation(x_hat[:, 0, b * N:(b + 1) * N], x_res[:, 0, b * N:(b + 1) * N], ACT.Identity,
                                         bias=gn[:, 4, b:b + 1], scale=gn[:, 3, b:b + 1]).then_inc(xhat_act, 1)

            nc.scalar.preload_act_table_set("natural_log_exp_and_others")
            act.wait_ge(consts_in, 16 * N_CONST)
            nc.scalar.activation(ident_neg[:], ident[:], ACT.Copy, scale=-1.0)
            normalise(0)
            for c in range(NCH + 3):
                if c < NCH:
                    act.wait_ge(xhat_act, BPC * (c + 1))
                    act.wait_ge(xhat_dve, BPC * (c + 1))
                    w = view(work, c * CH, [[T, H], [1, CH]])
                    nc.scalar.activation(w, x_hat[:, :, c * CH:(c + 1) * CH], ACT.Square).then_inc(sq_done, 1)
                if c < NCH:
                    act.wait_ge(n2_floor, c + 1)
                    power(rnorm, rnorm, rn_done)
                if 0 <= c - 1 < NCH:
                    for t in range(TPC):
                        i, hb = (c - 1) * TPC + t, t % 2
                        act.wait_ge(gram_done, i + 1)
                        if t == 0 and c == 1:
                            act.wait_ge(pool_init, 1)
                        if t == 0 and c - 1 >= 2:
                            act.wait_ge(gram_out[c - 3], 16)
                        off = GST + ((c - 1) % 2) * TPC * ROW + t * ROW + (0 if hb else REACH)
                        nc.scalar.activation(view(scratch, off, [[1, ROW - REACH]]), ps[:, 2 + i % 2, 0:ROW - REACH],
                                             ACT.Copy).then_inc(gram_row, 1)
                if 0 <= c - 3 < NCH:
                    d = c - 3
                    act.wait_ge(cor_tr, d + 1)
                    nc.scalar.activation(cor_t[:, d * CH:(d + 1) * CH], ps[0:NK, 4 + d % 2, :],
                                         ACT.Copy).then_inc(cor_t_done, 1)
                    for o in range(H):
                        act.wait_ge(y_done, H * d + o + 1)
                        if d >= 1:
                            act.wait_ge(x1_done, d)
                        nc.scalar.activation(view(scratch, YB + o * CH, [[1, CH]]), bank(6 + o), ACT.Relu,
                                             bias=conv_b_sb[:, o:o + 1]).then_inc(relu_done, 1)
            normalise(1)

            def second_part(n):
                s, c = n // NCH, n % NCH
                act.wait_ge(rest_done, n + 1)
                nc.scalar.activation(parts[:, s % 2, 1, c * CH:(c + 1) * CH], rest[:, n % 2], ACT.Copy).then_inc(part2, 1)

            for n in range(2 * H * NCH):
                s, c = n // NCH, n % NCH
                if c == 0 and s >= 2:
                    act.wait_ge(parts_out[s - 2], 16)
                act.wait_ge(qk_done, n + 1)
                nc.scalar.activation(parts[:, s % 2, 0, c * CH:(c + 1) * CH], bank(n % 4), ACT.Identity,
                                     bias=qk_bias_sb[:, s % 2:s % 2 + 1]).then_inc(part1, 1)
                if n >= 1:
                    second_part(n - 1)
            second_part(2 * H * NCH - 1)

            def fill_v(g):
                nc.scalar.activation(view(v_slot, 0, [[HPG * HPG * D, B * H], [HPG * D + D, HPG], [1, D]]),
                                     view(work, g * (HPG * D), [[C, B * H], [D, HPG], [1, D]]),
                                     ACT.Copy).then_inc(v_slot_ready, 1)

            def exponentials(U, u):
                act.wait_ge(sub_done, U + 1)
                if not isinstance(U, int) or U >= ER:
                    act.wait_ge(pv_done, U - ER + 1)
                nc.scalar.activation(e_ring[:, u % ER, :], ps[:, 2 * (u % 2):2 * (u % 2) + 2, :], ACT.Exp
                                     ).then_inc(exp_done, 1)

            def inverse(U, u):
                act.wait_ge(sum_done, U + 1)
                nc.scalar.activation(s_ln[:, u % 2], s_sum[:, u % 2], ACT.Ln).then_inc(ln_done, 1)
                act.wait_ge(ln_done, U + 1)
                if not isinstance(U, int) or U >= 2:
                    act.wait_ge(norm_done, U - 1)
                nc.scalar.activation(s_inv[:, u % 2], s_ln[:, u % 2], ACT.Exp, scale=-1.0).then_inc(r_done, 1)

            def evacuate(g):
                act.wait_ge(pv_done, g * UPG)
                nc.scalar.activation(o_sb[:], bank(4), ACT.Copy).then_inc(acc_out, 1)

            def attention(g, first):
                for u in range(UPG):
                    U = g * UPG + u
                    if u == LAG and not first:
                        evacuate(g)
                        fill_v(g)
                    if u >= 1 or not first:
                        exponentials(U - 1, u - 1)
                    if u >= 2 or not first:
                        inverse(U - 2, u - 2)

            act.wait_ge(v_stored, TILES)
            act.wait_ge(pool_init, 2)
            fill_v(0)
            attention(0, True)
            with act.Fori(1, NG) as g:
                attention(g, False)
            inverse(UNITS - 2, UPG - 2)
            exponentials(UNITS - 1, UPG - 1)
            inverse(UNITS - 1, UPG - 1)
            evacuate(NG)
            normalise(2)
            for b in range(B + 1):
                if b < B:
                    act.wait_ge(tr2_done, b + 1)
                    nc.scalar.activation(xt[:, b % 2], bank(b % 2), ACT.Copy).then_inc(xt_done, 1)
                    act.wait_ge(xx_done, b + 1)
                    if b >= 2:
                        act.wait_ge(o_done, b - 1)
                    nc.scalar.activation(xxt[:, b % 2], bank(2), ACT.Copy).then_inc(xx_out, 1)
            normalise(3)
            act.wait_ge(shifted, 1)
            nc.scalar.activation(route[:, 1], route[:, 0], ACT.Exp).then_inc(gate_exp, 1)

            def transposed(U, t):
                act.wait_ge(gtr_done, U + 1)
                if not isinstance(U, int) or U >= 2:
                    act.wait_ge(ye_done, U - 1)
                nc.scalar.activation(gated_t[:, t % 2], ps[:, 2 + t % 2, 0:C], ACT.Copy).then_inc(gt_done, 1)

            def experts(e, first):
                for t in range(TILES):
                    U = e * TILES + t
                    act.wait_ge(h_done, U + 1)
                    if t >= 2 or not first:
                        act.wait_ge(gated_done, U - 1)
                    nc.scalar.activation(gelu1[:, t % 2], ps[:, t % 2, 0:C], ACT.Gelu).then_inc(gelu_done, 1)
                    if t >= 1 or not first:
                        transposed(U - 1, t - 1)

            nc.scalar.preload_act_table(ACT.Gelu)
            experts(0, True)
            with act.Fori(1, E) as e:
                experts(e, False)
            transposed(E * TILES - 1, TILES - 1)

        @block.vector
        def _(dve):
            chain = [0]

            def count(ins):
                chain[0] += 1
                ins.then_inc(dve_chain, 1)

            def link(ins):
                count(ins)
                dve.wait_ge(dve_chain, chain[0])

            def group_norm(k, ready):
                for b in range(B):
                    ready(b)
                    for h in range(H):
                        count(nc.vector.bn_stats(stats[:, h * B + b], x_res[:, h, b * N:(b + 1) * N]))
                dve.wait_ge(dve_chain, chain[0])
                mean_e, mean_o, m2_e, m2_o = (stats[:, :, i] for i in (1, 4, 2, 5))
                count(nc.vector.tensor_tensor(gn[:, 5], mean_e, mean_e, ALU.mult))
                count(nc.vector.tensor_tensor(gn[:, 6], mean_o, mean_o, ALU.mult))
                count(nc.vector.tensor_tensor(gn[:, 7], m2_e, m2_o, ALU.add))
                link(nc.vector.tensor_tensor(sums[:, :, 0], mean_e, mean_o, ALU.add))
                link(nc.vector.tensor_tensor(gn[:, 5], gn[:, 5], gn[:, 6], ALU.add))
                nc.vector.scalar_tensor_tensor(out=sums[:, :, 1], in0=gn[:, 5], scalar=float(N // 2), in1=gn[:, 7],
                                               op0=ALU.mult, op1=ALU.add).then_inc(gn_sums, 1)
                dve.wait_ge(gn_group, k + 1)
                g = ps[:, 7, 0:2 * H * B].rearrange("p (j s) -> p j s", s=2)
                link(nc.vector.tensor_scalar(gn[:, 0], g[:, :, 0], 0.5 / GROUP, None, ALU.mult))
                link(nc.vector.tensor_tensor(gn[:, 1], gn[:, 0], gn[:, 0], ALU.mult))
                link(nc.vector.scalar_tensor_tensor(out=gn[:, 2], in0=g[:, :, 1], scalar=1.0 / (GROUP * N),
                                                    in1=gn[:, 1], op0=ALU.mult, op1=ALU.subtract))
                nc.vector.tensor_scalar(gn[:, 2], gn[:, 2], 0.0, EPS, ALU.max, ALU.add).then_inc(gn_var, 1)
                dve.wait_ge(gn_rstd, k + 1)
                link(nc.vector.tensor_tensor(gn[:, 5], gn[:, 3], gn[:, 3], ALU.mult))
                link(nc.vector.tensor_tensor(gn[:, 5], gn[:, 5], gn[:, 2], ALU.mult))
                link(nc.vector.tensor_scalar(gn[:, 5], gn[:, 5], -0.5, 1.5, ALU.mult, ALU.add))
                link(nc.vector.tensor_tensor(gn[:, 3], gn[:, 5], gn[:, 3], ALU.mult))
                nc.vector.scalar_tensor_tensor(out=gn[:, 4], in0=gn[:, 0], scalar=-1.0, in1=gn[:, 3],
                                               op0=ALU.mult, op1=ALU.mult).then_inc(gn_coef, 1)
                dve.wait_ge(gn_coef, k + 1)
                for b in range(B):
                    j = B + b
                    nc.vector.tensor_scalar(x_hat[:, 1, b * N:(b + 1) * N], x_res[:, 1, b * N:(b + 1) * N],
                                            gn[:, 3, j:j + 1], gn[:, 4, j:j + 1], ALU.mult, ALU.add
                                            ).then_inc(xhat_dve, 1)

            def x_loaded(b):
                if b % BPC == 0:
                    dve.wait_ge(x_in[b // BPC], 16 * H)

            group_norm(0, x_loaded)
            for c in range(NCH + 3):
                d = c - 3
                if c < NCH:
                    dve.wait_ge(n2_done, c + 1)
                    nc.vector.tensor_scalar(rnorm, bank(c % 2), EPS_NORM2, None, ALU.max).then_inc(n2_floor, 1)
                if 0 <= d < NCH:
                    dve.wait_ge(band_in[d], 16)
                    if d == 0:
                        dve.wait_ge(consts_in, 16 * N_CONST)
                    nc.vector.tensor_tensor(view(scratch, COR + d * TPC * NK, [[NK, TPC], [K, K], [1, K]]),
                                            view(scratch, BAND + d * TPC * WIN, [[WIN, TPC], [1, K], [SIDE, K]]),
                                            view(mask_sb, 0, [[0, TPC], [1, K], [0, K]]), ALU.mult).then_inc(cor_done, 1)
                if c < NCH:
                    dve.wait_ge(rn_done, c + 1)
                    w = view(work, c * CH, [[T, H], [1, CH]])
                    nc.vector.tensor_tensor(w, x_hat[:, :, c * CH:(c + 1) * CH], view(scratch, 0, [[0, H], [1, CH]]),
                                            ALU.mult).then_inc(fn_done, 1)
                    dve.wait_ge(fn_done, c + 1)
                if 0 <= d < NCH:
                    dve.wait_ge(relu_done, H * (d + 1))
                    xr = x_res[:, :, d * CH:(d + 1) * CH]
                    nc.vector.tensor_tensor(xr, xr, view(scratch, YB, [[CH, H], [1, CH]]), ALU.add).then_inc(x1_done, 1)

            group_norm(1, lambda b: dve.wait_ge(x1_done, b // BPC + 1))
            for n in range(2 * H * NCH):
                s, c = n // NCH, n % NCH
                dve.wait_ge(part1, n + 1)
                if n >= 2:
                    dve.wait_ge(part3, n - 1)
                nc.vector.scalar_tensor_tensor(out=rest[:, n % 2], in0=bank(n % 4), scalar=qk_bias_sb[:, s % 2:s % 2 + 1],
                                               in1=parts[:, s % 2, 0, c * CH:(c + 1) * CH], op0=ALU.add,
                                               op1=ALU.subtract).then_inc(rest_done, 1)
                dve.wait_ge(v_done, n + 1)
                nc.vector.tensor_tensor(v_all[:, n].rearrange("p (r d) -> p r d", d=D),
                                        ps[:, 4 + n % 2, 0:C].rearrange("p (r d) -> p r d", d=D),
                                        view(v_bias_sb, 0, [[0, HEADS], [1, D]]), ALU.add).then_inc(v_stored, 1)

            def maximum(U, u):
                dve.wait_ge(scores_done, U + 1)
                if not isinstance(U, int) or U >= 2:
                    dve.wait_ge(sub_done, U - 1)
                nc.vector.tensor_reduce(m_bf[:, u % 2], view(ps, 2 * (u % 2) * CH, [[1, P], [P, B]]), AX,
                                        ALU.max).then_inc(max_done, 1)

            def total(U, u):
                dve.wait_ge(exp_done, U + 1)
                if not isinstance(U, int) or U >= 2:
                    dve.wait_ge(r_done, U - 1)
                nc.vector.tensor_reduce(s_sum[:, u % 2], view(e_ring, (u % ER) * UW, [[1, P], [P, B]]), AX,
                                        ALU.add).then_inc(sum_done, 1)

            def add_heads(g, group):
                dve.wait_ge(acc_tr, group)
                xr = view(x_res, g * (HPG * D) - HPG * D, [[T, H], [N, B], [1, HPG * D]])
                nc.vector.tensor_tensor(xr, xr, view(ps, 5 * CH, [[N, H], [HPG * D, B], [1, HPG * D]]),
                                        ALU.add).then_inc(x2_added, 1)

            def attention(g, first):
                for u in range(UPG):
                    U = g * UPG + u
                    maximum(U, u)
                    if u >= 1 or not first:
                        total(U - 1, u - 1)
                    if u == LAG + 2 and not first:
                        add_heads(g, g)

            attention(0, True)
            with dve.Fori(1, NG) as g:
                attention(g, False)
            total(UNITS - 1, UPG - 1)
            add_heads(NG, NG)

            group_norm(2, lambda b: dve.wait_ge(x2_added, NG))
            for b in range(B + 1):
                if b < B:
                    dve.wait_ge(cx_done, b + 1)
                    if b >= 2:
                        dve.wait_ge(o_done, b - 1)
                    nc.vector.tensor_copy(cx[:, b % 2], ps[:, 3, :].rearrange("p (n c) -> p n c", n=2)).then_inc(cx_out, 1)
                if b >= 1:
                    dve.wait_ge(o_done, b)
                    dve.wait_ge(xsum_done, b)
                    xr = x_res[:, :, (b - 1) * N:b * N]
                    nc.vector.scalar_tensor_tensor(out=xr, in0=ps[:, 4 + (b - 1) % 2, :].rearrange("p (h n) -> p h n", h=H),
                                                   scalar=gamma_sb[:, 0:1], in1=xr, op0=ALU.mult, op1=ALU.add
                                                   ).then_inc(x3_done, 1)
            group_norm(3, lambda b: dve.wait_ge(x3_done, b + 1))

            def per_token(i):
                return route[:, i].rearrange("p (t e) -> p t e", e=E)

            def column(i):
                return view(scratch, COL + i * TILES, [[1, TILES], [0, E]])

            def col(i):
                return view(scratch, COL + i * TILES, [[1, TILES]])

            dve.wait_ge(logits_done, 1)
            lg = ps[:, 6, 0:TILES * E].rearrange("p (t e) -> p t e", e=E)
            link(nc.vector.tensor_reduce(col(0), lg, AX, ALU.max))
            nc.vector.tensor_tensor(per_token(0), lg, column(0), ALU.subtract).then_inc(shifted, 1)
            dve.wait_ge(gate_exp, 1)
            link(nc.vector.tensor_reduce(col(1), per_token(1), AX, ALU.add))
            link(nc.vector.reciprocal(col(2), col(1)))
            link(nc.vector.tensor_tensor(per_token(2), per_token(1), column(2), ALU.mult))

            def pick(prob, best, hot):
                link(nc.vector.tensor_reduce(col(best), per_token(prob), AX, ALU.max))
                link(nc.vector.tensor_tensor(per_token(3), per_token(prob), column(best), ALU.is_equal))
                link(nc.vector.tensor_tensor(per_token(3), per_token(3), view(rank_sb, 0, [[0, TILES], [1, E]]), ALU.mult))
                link(nc.vector.tensor_reduce(col(3), per_token(3), AX, ALU.max))
                link(nc.vector.tensor_tensor(per_token(hot), per_token(3), column(3), ALU.is_equal))

            pick(2, 4, 4)
            link(nc.vector.scalar_tensor_tensor(out=per_token(5), in0=per_token(4), scalar=-2.0, in1=per_token(2),
                                                op0=ALU.mult, op1=ALU.add))
            pick(5, 5, 6)
            link(nc.vector.tensor_tensor(col(6), col(4), col(5), ALU.add))
            link(nc.vector.reciprocal(col(7), col(6)))
            link(nc.vector.tensor_tensor(col(4), col(4), col(7), ALU.mult))
            link(nc.vector.tensor_tensor(col(5), col(5), col(7), ALU.mult))
            link(nc.vector.tensor_tensor(per_token(4), per_token(4), column(4), ALU.mult))
            link(nc.vector.tensor_tensor(per_token(6), per_token(6), column(5), ALU.mult))
            link(nc.vector.tensor_tensor(comb.rearrange("p (e t) -> p t e", e=E), per_token(4), per_token(6), ALU.add))
            dve.wait_ge(pool_init, 3)

            def add_expert(U, t, e):
                dve.wait_ge(ye_done, U + 1)
                nc.vector.scalar_tensor_tensor(out=y_acc[:, t % TILES], in0=ps[:, 4 + t % 2, 0:C],
                                               scalar=comb[:, bass.ds(e * TILES + t, 1)], in1=y_acc[:, t % TILES],
                                               op0=ALU.mult, op1=ALU.add).then_inc(ye_added, 1)

            def experts(e, first):
                for t in range(TILES):
                    U = e * TILES + t
                    dve.wait_ge(gelu_done, U + 1)
                    if t >= 2 or not first:
                        dve.wait_ge(gtr_done, U - 1)
                    nc.vector.tensor_tensor(gated[:, t % 2], ps[:, t % 2, C:2 * C], gelu1[:, t % 2],
                                            ALU.mult).then_inc(gated_done, 1)
                    if t >= 2 or not first:
                        add_expert(U - 2, t - 2, e)

            experts(0, True)
            with dve.Fori(1, E) as e:
                experts(e, False)
            for t in (TILES - 2, TILES - 1):
                add_expert((E - 1) * TILES + t, t, E - 1)
            for b in range(B):
                dve.wait_ge(ytr_done, b + 1)
                xr = x_res[:, :, b * N:(b + 1) * N]
                nc.vector.tensor_tensor(xr, xr, ps[:, b % 2, :].rearrange("p (h n) -> p h n", h=H), ALU.add
                                        ).then_inc(x4_done, 1)

        @block.tensor
        def _(pe):
            def group_norm(k):
                pe.wait_ge(gn_sums, k + 1)
                nc.tensor.matmul(ps[:, 7, 0:2 * H * B], group_sb[:], sums[:].rearrange("p j s -> p (j s)"),
                                 start=True, stop=True).then_inc(gn_group, 1)

            def normed(k, b):
                pe.wait_ge(xhat_act, B * k + b + 1)
                pe.wait_ge(xhat_dve, B * k + b + 1)

            pe.wait_ge(consts_in, 16 * N_CONST)
            group_norm(0)
            for c in range(NCH + 3):
                d = c - 3
                if c < NCH:
                    pe.wait_ge(sq_done, c + 1)
                    if c >= 2:
                        pe.wait_ge(n2_floor, c - 1)
                    for h in range(H):
                        last = nc.tensor.matmul(bank(c % 2), ones_sb[:], work[:, h * T + c * CH:h * T + (c + 1) * CH],
                                                start=(h == 0), stop=(h == H - 1))
                    last.then_inc(n2_done, 1)
                if 0 <= c - 1 < NCH:
                    pe.wait_ge(fn_done, c)
                    for t in range(TPC):
                        i, hb = (c - 1) * TPC + t, t % 2
                        if i >= 2:
                            pe.wait_ge(gram_row, i - 1)
                        q0 = (i // 2) * N + (P - REACH if hb else 0)
                        for h in range(H):
                            last = nc.tensor.matmul(ps[:, 2 + i % 2, 0:ROW - REACH], work[:, h * T + i * P:h * T + (i + 1) * P],
                                                    work[:, h * T + q0:h * T + q0 + ROW - REACH],
                                                    start=(h == 0), stop=(h == H - 1))
                        last.then_inc(gram_done, 1)
                if 0 <= d < NCH:
                    pe.wait_ge(cor_done, d + 1)
                    if d >= 2:
                        pe.wait_ge(cor_t_done, d - 1)
                    for t in range(TPC):
                        last = nc.tensor.transpose(ps[0:NK, 4 + d % 2, t * P:(t + 1) * P],
                                                   view(scratch, COR + (d * TPC + t) * NK, [[1, NK]]), ident[:])
                    last.then_inc(cor_tr, 1)
                    for o in range(H):
                        if d >= 1:
                            pe.wait_ge(relu_done, H * (d - 1) + o + 1)
                        for h in range(H):
                            nc.tensor.matmul(bank(6 + o), conv_wT_sb[:, h, o * P:(o + 1) * P],
                                             x_hat[:, h, d * CH:(d + 1) * CH], start=(h == 0), stop=False)
                        pe.wait_ge(cor_t_done, d + 1)
                        nc.tensor.matmul(bank(6 + o), conv_cT_sb[:, o * P:(o + 1) * P], cor_t[:, d * CH:(d + 1) * CH],
                                         start=False, stop=True).then_inc(y_done, 1)

            group_norm(1)
            for n in range(2 * H * NCH):
                s, c = n // NCH, n % NCH
                h = s // 2
                normed(1, BPC * (c + 1) - 1)
                if n >= 4:
                    pe.wait_ge(rest_done, n - 3)
                nc.tensor.matmul(bank(n % 4), qkv_sb[:, s % 2], x_hat[:, h, c * CH:(c + 1) * CH],
                                 start=True, stop=True).then_inc(qk_done, 1)
                normed(1, n // 2)
                if n >= 2:
                    pe.wait_ge(v_stored, n - 1)
                for h in range(H):
                    last = nc.tensor.matmul(ps[:, 4 + n % 2, h * P:(h + 1) * P], x_hat[:, h, n * P:(n + 1) * P],
                                            qkv_sb[:, 2], start=True, stop=True)
                last.then_inc(v_done, 1)

            def scores(U, u, g):
                i, mh, nh = u // 4, (u // 2) % 2, u % 2
                if u % 4 == 0:
                    pe.wait_ge(stack_in[i], (g + 1) * (2 * PARTS * 16))
                if not isinstance(U, int) or U >= 2:
                    pe.wait_ge(exp_done, U - 1)
                for b in range(B):
                    last = nc.tensor.matmul(ps[:, 2 * (u % 2) + b // 4, (b % 4) * P:(b % 4 + 1) * P],
                                            k_stack[:, i, b * N + mh * P:b * N + (mh + 1) * P],
                                            q_stack[:, i, b * N + nh * P:b * N + (nh + 1) * P],
                                            start=(b % 4 == 0), stop=(b % 4 == 3), skip_group_check=True)
                last.then_inc(scores_done, 1)

            def subtract(U, u):
                pe.wait_ge(max_done, U + 1)
                for j in range(2):
                    last = nc.tensor.matmul(bank(2 * (u % 2) + j), ident_neg[:],
                                            view(m_bf, (u % 2) * P, [[0, B // 2], [1, P]]), start=False, stop=True,
                                            skip_group_check=True)
                last.then_inc(sub_done, 1)

            def product(U, u, g):
                i, mh, nh = u // 4, (u // 2) % 2, u % 2
                if u == 0:
                    pe.wait_ge(v_slot_ready, g + 1)
                pe.wait_ge(norm_done, U + 1)
                for b in range(B):
                    last = nc.tensor.matmul(ps[32 * (b % 4):32 * (b % 4) + 32, 4, (b // 4) * N + nh * P:(b // 4) * N + (nh + 1) * P],
                                            v_slot[:, b * H + mh, i, :], e_ring[:, u % ER, b * P:(b + 1) * P],
                                            start=(u == 0 and b < 4), stop=(u == UPG - 1), skip_group_check=True)
                last.then_inc(pv_done, 1)

            def transpose_heads(group):
                pe.wait_ge(acc_out, group)
                if not isinstance(group, int) or group >= 2:
                    pe.wait_ge(x2_added, group - 1)
                for nh in range(H):
                    for j in range(2):
                        last = nc.tensor.transpose(ps[:, 5, (2 * nh + j) * P:(2 * nh + j + 1) * P],
                                                   o_sb[:, j * N + nh * P:j * N + (nh + 1) * P], ident[:])
                last.then_inc(acc_tr, 1)

            def attention(g, first):
                for u in range(UPG):
                    U = g * UPG + u
                    scores(U, u, g)
                    if u >= 1 or not first:
                        subtract(U - 1, (u - 1) % UPG)
                    if u >= LAG:
                        product(U - LAG, u - LAG, g)
                    elif not first:
                        product(U - LAG, u - LAG + UPG, g)
                    if u == LAG + 1 and not first:
                        transpose_heads(g)

            attention(0, True)
            with pe.Fori(1, NG) as g:
                attention(g, False)
            subtract(UNITS - 1, UPG - 1)
            for u in range(UPG - LAG, UPG):
                product((NG - 1) * UPG + u, u, NG - 1)
            transpose_heads(NG)

            group_norm(2)
            for b in range(B + 1):
                if b < B:
                    normed(2, b)
                    if b >= 2:
                        pe.wait_ge(xt_done, b - 1)
                    for nh in range(2):
                        for h in range(H):
                            last = nc.tensor.transpose(ps[:, b % 2, nh * C + h * P:nh * C + (h + 1) * P],
                                                       x_hat[:, h, b * N + nh * P:b * N + (nh + 1) * P], ident[:])
                    last.then_inc(tr2_done, 1)
                    if b >= 1:
                        pe.wait_ge(cx_out, b)
                    for o in range(H):
                        for h in range(H):
                            last = nc.tensor.matmul(ps[:, 3, o * N:(o + 1) * N], gram_wT_sb[:, h, o * P:(o + 1) * P],
                                                    x_hat[:, h, b * N:(b + 1) * N], start=(h == 0), stop=(h == H - 1))
                    last.then_inc(cx_done, 1)
                if b >= 1:
                    a = b - 1
                    pe.wait_ge(xx_out, a + 1)
                    pe.wait_ge(cx_out, a + 1)
                    if a >= 2:
                        pe.wait_ge(x3_done, a - 1)
                    for o in range(H):
                        for h in range(H):
                            last = nc.tensor.matmul(ps[:, 4 + a % 2, o * N:(o + 1) * N], xxt[:, a % 2, h, o * P:(o + 1) * P],
                                                    cx[:, a % 2, h, :], start=(h == 0), stop=(h == H - 1))
                    last.then_inc(o_done, 1)
                if b < B:
                    pe.wait_ge(xt_done, b + 1)
                    if b >= 1:
                        pe.wait_ge(xx_out, b)
                    for o in range(H):
                        for n in range(2):
                            last = nc.tensor.matmul(ps[:, 2, o * C:(o + 1) * C], xt[:, b % 2, n, o * P:(o + 1) * P],
                                                    xt[:, b % 2, n, :], start=(n == 0), stop=(n == 1))
                    last.then_inc(xx_done, 1)

            group_norm(3)
            for t in range(TILES):
                normed(3, t // 2)
                for h in range(H):
                    last = nc.tensor.matmul(ps[:, 6, t * E:(t + 1) * E], x_hat[:, h, t * P:(t + 1) * P], gate_sb[:, h],
                                            start=(h == 0), stop=(h == H - 1))
            last.then_inc(logits_done, 1)
            pe.wait_ge(w_in, 64)

            def up(U, t, e, first):
                if t >= 2 or not first:
                    pe.wait_ge(gated_done, U - 1)
                for h in range(H):
                    last = nc.tensor.matmul(bank(t % 2), x_hat[:, h, t * P:(t + 1) * P],
                                            w13_sb[:, h, bass.ds(e * (2 * C), 2 * C)], start=(h == 0), stop=(h == H - 1))
                last.then_inc(h_done, 1)

            def turn(U, t, first):
                pe.wait_ge(gated_done, U + 1)
                if not first:
                    pe.wait_ge(gt_done, U - 1)
                for f in range(2):
                    last = nc.tensor.transpose(ps[:, 2 + t % 2, f * P:(f + 1) * P], gated[:, t % 2, f * P:(f + 1) * P], ident[:])
                last.then_inc(gtr_done, 1)

            def down(U, t, e, first):
                pe.wait_ge(gt_done, U + 1)
                if not first:
                    pe.wait_ge(ye_added, U - 1)
                for f in range(2):
                    last = nc.tensor.matmul(ps[:, 4 + t % 2, 0:C], gated_t[:, t % 2, f * P:(f + 1) * P],
                                            w2_sb[:, f, bass.ds(e * C, C)], start=(f == 0), stop=(f == 1))
                last.then_inc(ye_done, 1)

            def experts(e, first):
                for t in range(TILES):
                    U = e * TILES + t
                    up(U, t, e, first)
                    if t >= 1 or not first:
                        turn(U - 1, t - 1, first and t < 3)
                    if t >= 2:
                        down(U - 2, t - 2, e, first and t < 4)
                    elif not first:
                        down(U - 2, t - 2, e - 1, False)

            experts(0, True)
            with pe.Fori(1, E) as e:
                experts(e, False)
            U = E * TILES
            turn(U - 1, TILES - 1, False)
            down(U - 2, TILES - 2, E - 1, False)
            down(U - 1, TILES - 1, E - 1, False)
            pe.wait_ge(ye_added, U)
            for b in range(B):
                if b >= 2:
                    pe.wait_ge(x4_done, b - 1)
                for h in range(H):
                    for nh in range(2):
                        last = nc.tensor.transpose(ps[:, b % 2, h * N + nh * P:h * N + (nh + 1) * P],
                                                   y_acc[:, 2 * b + nh, h * P:(h + 1) * P], ident[:])
                last.then_inc(ytr_done, 1)


def _arrays(x, L0_conv_conv_w, L0_conv_conv_b, L1_conv_w_qkv, L1_conv_b_qkv, L2_conv_W, L2_conv_gamma,
            L3_conv_gate_w, L3_conv_w1, L3_conv_w2, L3_conv_w3):
    import numpy as np
    f = np.float32
    C, P, D, S, K = 256, 128, 8, 16, 5
    E = L3_conv_w1.shape[0]
    conv_w = np.asarray(L0_conv_conv_w)
    w_qkv, b_qkv = np.asarray(L1_conv_w_qkv), np.asarray(L1_conv_b_qkv)
    blocks = np.zeros((3, P, P), f)
    for s in range(3):
        for r in range(P // D):
            blocks[s, r * D:(r + 1) * D, r * D:(r + 1) * D] = w_qkv[s * D:(s + 1) * D].T
    w13T = np.stack([np.asarray(L3_conv_w1), np.asarray(L3_conv_w3)], 1)
    col = np.arange(P) % S
    shift = np.arange(K) - K // 2
    inside = (col[:, None] + shift[None] >= 0) & (col[:, None] + shift[None] < S)
    group = np.arange(P) // 8
    return {
        "x": np.asarray(x),
        "conv_wT": conv_w[:, :C].T.reshape(2, P, C),
        "conv_cT": conv_w[:, C:].T,
        "conv_b": np.asarray(L0_conv_conv_b).reshape(2, P).T,
        "qkv_blocks": blocks,
        "qk_bias": np.stack([np.tile(b_qkv[:D], P // D), np.tile(b_qkv[D:2 * D], P // D)], 1),
        "v_bias": np.broadcast_to(b_qkv[2 * D:], (P, D)),
        "gram_wT": np.asarray(L2_conv_W).T.reshape(2, P, C),
        "gamma": np.broadcast_to(np.asarray(L2_conv_gamma).reshape(1, 1), (P, 1)),
        "gate_wT": np.asarray(L3_conv_gate_w).T,
        "w13T": w13T.transpose(3, 0, 1, 2).reshape(2, P, E * 2 * C),
        "w2T": np.asarray(L3_conv_w2).transpose(2, 0, 1).reshape(2, P, E * C),
        "identity": np.eye(P, dtype=f),
        "ones": np.ones((P, P), f),
        "group_ones": (group[:, None] == group[None]).astype(f),
        "edge_mask": inside.astype(f),
        "expert_rank": np.broadcast_to(np.arange(E, 0, -1).astype(f), (P, E)),
    }


def kernel(**inputs):
    import numpy as _np
    import concourse.bacc as _bacc
    from concourse import mybir as _mybir
    from concourse.bass_utils import run_bass_kernel_spmd as _run

    nc = _bacc.Bacc("TRN2", target_bir_lowering=False, num_devices=1)
    arrays, args = {}, []
    for name, a in _arrays(**inputs).items():
        a = _np.ascontiguousarray(a)
        arrays[f"in_{name}_dram"] = a
        args.append(nc.dram_tensor(f"in_{name}_dram", a.shape, _mybir.dt.from_np(a.dtype), kind="ExternalInput").ap())
    shape = tuple(inputs["x"].shape)
    args.append(nc.dram_tensor("out_0_dram", shape, _mybir.dt.float32, kind="ExternalOutput").ap())
    conv_stack_kernel(nc, *args)
    r = _run(nc, [arrays], core_ids=[0])
    return r.results[0]["out_0_dram"]
```

```python
import concourse.bass as bass
from concourse import mybir
from contextlib import ExitStack


def conv_stack_kernel(nc, x, conv_wT, conv_cT, conv_b, qkv_blocks, qk_bias, v_bias, gram_wT, gamma,
                      gate_wT, w13T, w2T, identity, ones, group_ones, edge_mask, expert_rank,
                      before, tables,
                      out):
    fp32, bf16 = mybir.dt.float32, mybir.dt.bfloat16
    ALU, ACT, AX = mybir.AluOpType, mybir.ActivationFunctionType, mybir.AxisListType.X

    B, C, SIDE = x.shape[0], x.shape[1], x.shape[2]
    N = SIDE * SIDE
    P = 128
    H = C // P
    T = B * N
    TILES = T // P
    CH = 512
    NCH = T // CH
    BPC = CH // N
    GROUP = 8
    K = 5
    NK = K * K
    REACH = (K // 2) * (SIDE + 1)
    WIN = 2 * REACH + 1
    ROW = P + 2 * REACH
    HEADS, D = 32, C // 32
    PARTS = 3
    KR = PARTS * PARTS * D
    HPG = 4
    NG = HEADS // HPG
    UPG = HPG * 4
    UNITS = NG * UPG
    UW = B * P
    ER = 8
    LAG = 4
    E = gate_wT.shape[1]
    TOP = 2
    PAIRS = TOP * TILES
    SLOTS = (TOP * T + E * (P - 1)) // P
    YROWS = T + P
    EPS = 1e-5
    ROUND = 1.5 * 2.0 ** 23
    EPS_NORM2 = 1e-24

    gram_dram = nc.dram_tensor("gram_rows", (TILES, P, ROW), fp32, kind="Internal").ap()
    part_dram = nc.dram_tensor("qk_parts", (2, PARTS, C, T), bf16, kind="Internal").ap()
    row_dram = nc.dram_tensor("token_rows", (YROWS, C + E), fp32, kind="Internal").ap()
    y_dram = nc.dram_tensor("expert_sums", (YROWS, C), fp32, kind="Internal").ap()

    ctx = ExitStack()
    with ctx:
        def sb(name, shape, dt=fp32):
            return ctx.enter_context(nc.sbuf_tensor(name, shape, dt))

        def sem(name):
            return ctx.enter_context(nc.semaphore(name))

        def view(t, off, dims, rows=P):
            width = 1
            for s in t.shape[1:]:
                width *= s
            return bass.AP(t, off, [[width, rows]] + [list(d) for d in dims])

        x_res = sb("x_res", [P, H, T])
        x_hat = sb("x_hat", [P, H, T])
        work = sb("work", [P, H * T])
        e_ring = sb("e_ring", [P, ER, UW])
        scratch = sb("scratch", [P, 6144])
        q_stack = sb("q_stack", [KR, HPG, T], bf16)
        k_stack = sb("k_stack", [KR, HPG, T], bf16)
        v_slot = sb("v_slot", [P, B * H, HPG, HPG * D])
        w13_sb = sb("w13_sb", [P, H, E * 2 * C])
        w2_sb = sb("w2_sb", [P, H, E * C])
        conv_wT_sb = sb("conv_wT_sb", [P, H, C])
        conv_cT_sb = sb("conv_cT_sb", [NK, C])
        conv_b_sb = sb("conv_b_sb", [P, H])
        qkv_sb = sb("qkv_sb", [P, 3, P])
        qk_bias_sb = sb("qk_bias_sb", [P, 2])
        v_bias_sb = sb("v_bias_sb", [P, D])
        gram_wT_sb = sb("gram_wT_sb", [P, H, C])
        gamma_sb = sb("gamma_sb", [P, 1])
        gate_sb = sb("gate_sb", [P, H, E])
        ident = sb("ident", [P, P])
        ident_neg = sb("ident_neg", [P, P], bf16)
        ones_sb = sb("ones_sb", [P, P])
        group_sb = sb("group_sb", [P, P])
        mask_sb = sb("mask_sb", [P, K])
        rank_sb = sb("rank_sb", [P, E])
        before_sb = sb("before_sb", [P, P])
        before_bf = sb("before_bf", [P, P], bf16)
        ones_bf = sb("ones_bf", [P, P], bf16)
        mask_bf = sb("mask_bf", [P, TILES, E], bf16)
        NUM, KNUM, TILE0, PLACE, PAD = 0, P, P + SLOTS, P + SLOTS + PAIRS, P + SLOTS + PAIRS + 1
        tab = sb("tab", [P, PAD + 1])
        slot_x = sb("slot_x", [P, SLOTS], mybir.dt.uint32)
        slot_e = sb("slot_e", [P, SLOTS + 1], mybir.dt.int32)
        SPC = H * BPC
        stats = sb("stats", [P, NCH, SPC, 6])
        gn = sb("gn", [P, NCH, 4, SPC])
        gn_tmp = sb("gn_tmp", [P, SPC])
        m_bf = sb("m_bf", [P, 2, P], bf16)
        s_sum = sb("s_sum", [P, 2, P])
        s_ln = sb("s_ln", [P, 2, P])
        s_inv = sb("s_inv", [P, 2, P])
        ps = ctx.enter_context(nc.psum_tensor("ps", [P, 8, CH], fp32))

        TPC = CH // P
        rnorm = scratch[:, 0:CH]
        GST = CH
        BAND = GST + 2 * TPC * ROW
        COR = BAND + TILES * WIN
        YB = COR + TILES * NK
        cor_t = view(e_ring, 0, [[1, T]], rows=NK)
        o_sb = scratch[:, 0:CH]
        parts = scratch[:, :].bitcast(bf16).rearrange("p (s a t) -> p s a t", s=2, a=PARTS)
        rest = e_ring[:, 2:3, :].rearrange("p a (s c) -> p (a s) c", s=2)
        xt = e_ring[:, 0, :].rearrange("p (s n c) -> p s n c", s=2, n=2)
        xxt = e_ring[:, 1, :].rearrange("p (s n c) -> p s n c", s=2, n=2)
        cx = e_ring[:, 2, :].rearrange("p (s n c) -> p s n c", s=2, n=2)
        rows = work[:, :].rearrange("p (t c) -> p t c", t=TILES)
        SEC = PAIRS * SLOTS
        hot_lo = e_ring[:, 0:2, :].rearrange("p a b -> p (a b)").bitcast(bf16).rearrange("p (j n) -> p j n", j=PAIRS)
        hot_hi = e_ring[:, 2:4, :].rearrange("p a b -> p (a b)").bitcast(bf16)[:, 0:3 * SEC].rearrange(
            "p (s j k) -> p s j k", s=3, j=PAIRS)
        XR = 8
        x_rows = view(e_ring, 5 * UW, [[C + E, XR], [1, C + E]])
        x_turned = view(e_ring, 4 * UW, [[C, 2], [1, C]])
        gelu1 = view(e_ring, 4 * UW + 2 * C, [[C, 2], [1, C]])
        gated = view(scratch, 4096, [[C, 2], [1, C]])
        gated_t = view(scratch, 4096 + 2 * C, [[C, 2], [1, C]])
        y_rows = view(scratch, 4096 + 4 * C, [[C, 4], [1, C]])
        y_back = work[:, :].rearrange("p (t c) -> p t c", t=TILES)
        COL = 11 * TILES * E
        POS, HI, LO = (COL + 128 + i * PAIRS for i in range(3))
        START = COL + 128 + 3 * PAIRS
        TILE_N = START + 4 * E
        OWN = TILE_N + E
        EXPERT = OWN + SLOTS * E
        EMPTY = EXPERT + SLOTS
        GATE = EMPTY + SLOTS
        OWN_GATE = GATE + SLOTS
        RANK = 32
        HUGE = 3.0e38
        v_all = work[:, :].rearrange("p (t c) -> p t c", t=TILES)

        GN_BANK = (5, 5, 7, 7)

        def bank(i):
            return ps[:, i, :]

        def s_view(off, *dims):
            return view(scratch, off, dims)

        x_in = [sem(f"x_in{c}") for c in range(NCH)]
        first_in, conv_in, consts_in, w_in = sem("first_in"), sem("conv_in"), sem("consts_in"), sem("w_in")
        pool_init = sem("pool_init")
        gn_sums = [sem(f"gn_sums{k}") for k in range(4)]
        gn_group, gn_var, gn_rstd, gn_coef = (sem("gn_" + n) for n in ("group", "var", "rstd", "coef"))
        xhat_act, xhat_dve = sem("xhat_act"), sem("xhat_dve")
        dve_chain, act_chain = sem("dve_chain"), sem("act_chain")
        sq_done, n2_done, n2_floor, rn_done, fn_done = (sem(n) for n in ("sq_done", "n2_done", "n2_floor", "rn_done", "fn_done"))
        gram_done, gram_row = sem("gram_done"), sem("gram_row")
        gram_out = [sem(f"gram_out{c}") for c in range(NCH)]
        band_in = [sem(f"band_in{c}") for c in range(NCH)]
        parts_out = [sem(f"parts_out{n}") for n in range(4 * H)]
        cor_done, cor_tr, cor_t_done, y_done, relu_done, x1_done = (
            sem(n) for n in ("cor_done", "cor_tr", "cor_t_done", "y_done", "relu_done", "x1_done"))
        qk_done, part1, rest_done, part2, part3 = (
            sem(n) for n in ("qk_done", "part1", "rest_done", "part2", "part3"))
        v_done, v_stored = sem("v_done"), sem("v_stored")
        stack_in = [sem(f"stack_in{i}") for i in range(HPG)]
        scores_done, max_done, sub_done, exp_done, sum_done, ln_done, r_done, norm_done, pv_done = (
            sem(n) for n in ("scores_done", "max_done", "sub_done", "exp_done", "sum_done", "ln_done", "r_done",
                             "norm_done", "pv_done"))
        acc_out, v_slot_ready, acc_tr, x2_added = (sem(n) for n in ("acc_out", "v_slot_ready", "acc_tr", "x2_added"))
        tr2_done, xt_done, cx_done, cx_out, xx_done, xx_out, o_done, x3_done, xsum_done = (
            sem(n) for n in ("tr2_done", "xt_done", "cx_done", "cx_out", "xx_done", "xx_out", "o_done", "x3_done",
                             "xsum_done"))
        logits_done, logits_read, shifted, gate_exp, comb_done, gate_own, gate_done = (
            sem(n) for n in ("logits_done", "logits_read", "shifted", "gate_exp", "comb_done", "gate_own", "gate_done"))
        h_done, gelu_done, gated_done, gtr_done, gt_done, ye_done, ye_out = (
            sem(n) for n in ("h_done", "gelu_done", "gated_done", "gtr_done", "gt_done", "ye_done", "ye_out"))
        rtr_done, row_done, row_out, zero_out = sem("rtr_done"), sem("row_done"), sem("row_out"), sem("zero_out")
        mask_done, ranks_done, places_done, tiles_hot, tiles_scaled, hots_done, slots_done, plan_done = (
            sem(n) for n in ("mask_done", "ranks_done", "places_done", "tiles_hot", "tiles_scaled", "hots_done",
                             "slots_done", "plan_done"))
        xr_in = [sem(f"xr_in{i}") for i in range(XR)]
        y_out = sem("y_out")
        xtr_done, xt_out = sem("xtr_done"), sem("xt_out")
        y_in = [sem(f"y_in{i}") for i in range(NCH)]
        ytr_done, x4_done, out_done = sem("ytr_done"), sem("x4_done"), sem("out_done")

        def slot_steps(eng, step):
            inside = lambda k: not isinstance(k, int) or 0 <= k < SLOTS
            for s in range(7):
                step(s, s, inside)
            with eng.Fori(0, (SLOTS - 7) // XR) as i:
                for r in range(7, 7 + XR):
                    step(i * XR + r, r % XR, inside)
            for s in range(SLOTS, SLOTS + 3):
                step(s, s % XR, inside)

        assert (SLOTS - 7) % XR == 0
        block = ctx.enter_context(nc.Block())
        FIRST, CONV, LATER = 3, 4, 9

        @block.sync
        def _(sp):
            for c in range(NCH):
                for h in range(H):
                    sp.dma_start(x_res[:, h, c * CH:(c + 1) * CH].rearrange("p (b n) -> p b n", b=BPC),
                                 x[c * BPC:(c + 1) * BPC, h * P:(h + 1) * P].rearrange("b p y x -> p b (y x)")
                                 ).then_inc(x_in[c], 16)
                if c == 0:
                    for dst, src in ((conv_wT_sb[:], conv_wT.rearrange("h p o -> p h o")), (mask_sb[:], edge_mask),
                                     (conv_cT_sb[:], conv_cT), (conv_b_sb[:], conv_b)):
                        sp.dma_start(dst, src).then_inc(conv_in, 16)
            later = ((qkv_sb[:], qkv_blocks.rearrange("s p o -> p s o")), (qk_bias_sb[:], qk_bias), (v_bias_sb[:], v_bias),
                     (gram_wT_sb[:], gram_wT.rearrange("h p o -> p h o")), (gamma_sb[:], gamma),
                     (gate_sb[:], gate_wT.rearrange("(h p) e -> p h e", p=P)), (rank_sb[:], expert_rank),
                     (before_sb[:], before), (tab[:], tables))
            for dst, src in later:
                sp.dma_start(dst, src).then_inc(consts_in, 16)
            sp.wait_ge(pool_init, 2)
            zeros = v_slot[:, :].rearrange("p a h d -> p (a h d)")
            sp.dma_start(row_dram[T:YROWS], zeros[:, 0:C + E]).then_inc(zero_out, 16)
            sp.dma_start(y_dram[T:YROWS], zeros[:, 0:C]).then_inc(zero_out, 16)
            for i in range(2):
                sp.dma_start(y_dram[i * T // 2:(i + 1) * T // 2].rearrange("(p r) c -> p (r c)", p=P), zeros).then_inc(zero_out, 16)
            for c in range(NCH):
                sp.wait_ge(gram_row, TPC * (c + 1))
                sp.dma_start(gram_dram[c * TPC:(c + 1) * TPC].rearrange("t p r -> p t r"),
                             view(scratch, GST + (c % 2) * TPC * ROW, [[ROW, TPC], [1, ROW]])
                             ).then_inc(gram_out[c], 16)
                sp.wait_ge(gram_out[c], 16)
                skew = bass.AP(gram_dram.tensor, c * TPC * P * ROW, [[ROW + 1, P], [P * ROW, TPC], [1, WIN]])
                sp.dma_start(view(scratch, BAND + c * TPC * WIN, [[WIN, TPC], [1, WIN]]), skew
                             ).then_inc(band_in[c], 16)

            def load_stack(g, i):
                row = (g * HPG + i) * D * T
                for a in range(PARTS):
                    rows_a = slice(a * PARTS * D, (a + 1) * PARTS * D)
                    q_src = bass.AP(part_dram.tensor, row, [[C * T, PARTS], [T, D], [1, T]])
                    k_src = bass.AP(part_dram.tensor, row + (PARTS + a) * C * T, [[0, PARTS], [T, D], [1, T]])
                    sp.dma_start(q_stack[rows_a, i, :], q_src).then_inc(stack_in[i], 16)
                    sp.dma_start(k_stack[rows_a, i, :], k_src).then_inc(stack_in[i], 16)

            for n in range(4 * H):
                sp.wait_ge(part3, NCH // 2 * (n + 1))
                h, s, cols = n // 4, n // 2 % 2, slice(n % 2 * (T // 2), (n % 2 + 1) * (T // 2))
                dst = bass.AP(part_dram.tensor, (s * PARTS * C + h * P) * T + n % 2 * (T // 2), [[T, P], [C * T, PARTS], [1, T // 2]])
                sp.dma_start(dst, parts[:, s, :, cols]).then_inc(parts_out[n], 16)
                if n == 3:
                    for i in range(4):
                        sp.wait_ge(parts_out[i], 16)
                    for i in range(HPG):
                        load_stack(0, i)
            for n in range(4, 8):
                sp.wait_ge(parts_out[n], 16)
            for h in range(H):
                sp.dma_start(w13_sb[:, h, :], w13T[h]).then_inc(w_in, 16)
                sp.dma_start(w2_sb[:, h, :], w2T[h]).then_inc(w_in, 16)
            with sp.Fori(0, NG - 1) as g:
                for i in range(HPG):
                    sp.wait_ge(scores_done, g * UPG + 4 * (i + 1))
                    load_stack(g + 1, i)
            for c in range(NCH):
                sp.wait_ge(row_done, BPC * (c + 1))
                sp.dma_start(row_dram[c * CH:(c + 1) * CH, 0:C].rearrange("(t p) c -> p t c", p=P),
                             rows[:, c * TPC:(c + 1) * TPC]).then_inc(row_out, 16)
            sp.wait_ge(comb_done, 1)
            sp.dma_start(row_dram[0:T, C:C + E].rearrange("(t p) e -> p t e", p=P),
                         s_view(7 * TILES * E, [E, TILES], [1, E])).then_inc(row_out, 16)
            sp.wait_ge(y_out, 16 * SLOTS)
            for c in range(NCH):
                sp.dma_start(y_back[:, c * TPC:(c + 1) * TPC],
                             y_dram[c * CH:(c + 1) * CH].rearrange("(t p) c -> p t c", p=P)).then_inc(y_in[c], 16)
            for b in range(B):
                sp.wait_ge(x4_done, b + 1)
                sp.dma_start(out[b].rearrange("(h p) y x -> p h (y x)", p=P),
                             x_res[:, :, b * N:(b + 1) * N]).then_inc(out_done, 16)
            sp.wait_ge(out_done, 16 * B)

        @block.gpsimd
        def _(pool):
            nc.gpsimd.memset(view(scratch, GST, [[1, 2 * TPC * ROW]]), 0.0).then_inc(pool_init, 1)
            nc.gpsimd.memset(v_slot[:], 0.0).then_inc(pool_init, 1)
            pool.wait_ge(pool_init, 2)
            for n in range(2 * H * NCH):
                s, c = n // NCH, n % NCH
                pool.wait_ge(part2, n + 1)
                nc.gpsimd.tensor_tensor(parts[:, s % 2, 2, c * CH:(c + 1) * CH], rest[:, n % 2],
                                        parts[:, s % 2, 1, c * CH:(c + 1) * CH], ALU.subtract).then_inc(part3, 1)
            with pool.Fori(0, NG) as g:
                for u in range(UPG):
                    pool.wait_ge(r_done, g * UPG + u + 1)
                    ev = e_ring[:, u % ER, :].rearrange("p (b n) -> p b n", b=B)
                    nc.gpsimd.tensor_tensor(ev, ev, view(s_inv, (u % 2) * P, [[0, B], [1, P]]),
                                            ALU.mult).then_inc(norm_done, 1)
            for b in range(B):
                pool.wait_ge(xhat_act, B * 2 + b + 1)
                pool.wait_ge(xhat_dve, B * 2 + b + 1)
                nc.gpsimd.tensor_tensor(x_res[:, :, b * N:(b + 1) * N], x_res[:, :, b * N:(b + 1) * N],
                                        x_hat[:, :, b * N:(b + 1) * N], ALU.add).then_inc(xsum_done, 1)
            pool.wait_ge(tiles_hot, 1)
            nc.gpsimd.tensor_tensor(hot_hi[:, 0], hot_hi[:, 2], view(tab, TILE0, [[1, PAIRS], [0, SLOTS]]),
                                    ALU.mult).then_inc(tiles_scaled, 1)
            pool.wait_ge(plan_done, 1)
            pool.wait_ge(row_out, 16 * (NCH + 1))
            pool.wait_ge(zero_out, 16 * 4)

            def gather(k):
                if k >= XR:
                    pool.wait_ge(xtr_done, k - XR + 1)
                    pool.wait_ge(gate_done, k - XR + 1)
                nc.gpsimd.indirect_dma_start(out=x_rows[:, k % XR], out_offset=None, in_=row_dram[:, :],
                                             in_offset=bass.IndirectOffsetOnAxis(ap=slot_x[:, k:k + 1], axis=0)
                                             ).then_inc(xr_in[k % XR], 16)

            for k in range(XR):
                gather(k)
            for k in range(SLOTS):
                pool.wait_ge(ye_out, k + 1)
                if k >= 1:
                    pool.wait_ge(y_out, 16 * k)
                nc.gpsimd.indirect_dma_start(out=y_dram[:, :], in_=y_rows[:, k % 4], in_offset=None,
                                             out_offset=bass.IndirectOffsetOnAxis(ap=slot_x[:, k:k + 1], axis=0),
                                             compute_op=ALU.add).then_inc(y_out, 16)
                if k + XR < SLOTS:
                    gather(k + XR)

        @block.scalar
        def _(act):
            chain = [0]

            def link(ins):
                chain[0] += 1
                ins.then_inc(act_chain, 1)
                act.wait_ge(act_chain, chain[0])

            for dst, src in ((group_sb[:], group_ones), (ones_sb[:], ones), (ident[:], identity)):
                act.dma_start(dst, src).then_inc(first_in, 16)

            def power(dst, src, done):
                link(nc.scalar.activation(dst, src, ACT.Ln))
                nc.scalar.activation(dst, dst, ACT.Exp, scale=-0.5).then_inc(done, 1)

            def deviation(k, c):
                act.wait_ge(gn_var, NCH * k + c + 1)
                power(gn[:, c, 2], gn[:, c, 1], gn_rstd)

            def normalise(k, c):
                act.wait_ge(gn_coef, NCH * k + c + 1)
                for i in range(BPC):
                    cols = slice((c * BPC + i) * N, (c * BPC + i + 1) * N)
                    nc.scalar.activation(x_hat[:, 0, cols], x_res[:, 0, cols], ACT.Identity,
                                         bias=gn[:, c, 3, i:i + 1], scale=gn[:, c, 2, i:i + 1]).then_inc(xhat_act, 1)

            nc.scalar.preload_act_table_set("natural_log_exp_and_others")
            act.wait_ge(first_in, 16 * FIRST)
            nc.scalar.activation(ident_neg[:], ident[:], ACT.Copy, scale=-1.0)

            def squares_of(c):
                act.wait_ge(xhat_act, BPC * (c + 1))
                act.wait_ge(xhat_dve, BPC * (c + 1))
                nc.scalar.activation(view(work, c * CH, [[T, H], [1, CH]]), x_hat[:, :, c * CH:(c + 1) * CH],
                                     ACT.Square).then_inc(sq_done, 1)

            def gram_rows(c):
                for t in range(TPC):
                    i, hb = c * TPC + t, t % 2
                    act.wait_ge(gram_done, i + 1)
                    if i == 0:
                        act.wait_ge(pool_init, 1)
                    if t == 0 and c >= 2:
                        act.wait_ge(gram_out[c - 2], 16)
                    off = GST + (c % 2) * TPC * ROW + t * ROW + (0 if hb else REACH)
                    nc.scalar.activation(view(scratch, off, [[1, ROW - REACH]]), ps[:, 2 + i % 2, 0:ROW - REACH],
                                         ACT.Copy).then_inc(gram_row, 1)

            def turned_correlations(d):
                act.wait_ge(cor_tr, d + 1)
                nc.scalar.activation(cor_t[:, d * CH:(d + 1) * CH], ps[0:NK, 4, :], ACT.Copy).then_inc(cor_t_done, 1)

            def conv_out(d):
                if d == 0:
                    act.wait_ge(conv_in, 16 * CONV)
                for o in range(H):
                    act.wait_ge(y_done, H * d + o + 1)
                    if d >= 1:
                        act.wait_ge(x1_done, d)
                    nc.scalar.activation(view(scratch, YB + o * CH, [[1, CH]]), bank(6 + o), ACT.Relu,
                                         bias=conv_b_sb[:, o:o + 1]).then_inc(relu_done, 1)

            deviation(0, 0)
            normalise(0, 0)
            squares_of(0)
            for t in range(NCH + 2):
                if t < NCH:
                    act.wait_ge(n2_floor, t + 1)
                    power(rnorm, rnorm, rn_done)
                if t + 1 < NCH:
                    deviation(0, t + 1)
                    normalise(0, t + 1)
                    squares_of(t + 1)
                if t < NCH:
                    gram_rows(t)
                if 0 <= t - 1 < NCH:
                    turned_correlations(t - 1)
                if 0 <= t - 2:
                    deviation(1, t - 2)
                    normalise(1, t - 2)
                if 0 <= t - 1 < NCH:
                    conv_out(t - 1)
            act.wait_ge(consts_in, 16 * LATER)
            nc.scalar.activation(before_bf[:], before_sb[:], ACT.Copy).then_inc(act_chain, 1)
            nc.scalar.activation(ones_bf[:], ones_sb[:], ACT.Copy).then_inc(act_chain, 1)
            chain[0] += 2
            def second_part(n):
                s, c = n // NCH, n % NCH
                act.wait_ge(rest_done, n + 1)
                nc.scalar.activation(parts[:, s % 2, 1, c * CH:(c + 1) * CH], rest[:, n % 2], ACT.Copy).then_inc(part2, 1)

            for n in range(2 * H * NCH):
                s, c = n // NCH, n % NCH
                if c % 2 == 0 and s >= 2:
                    act.wait_ge(parts_out[2 * (s - 2) + c // 2], 16)
                act.wait_ge(qk_done, n + 1)
                nc.scalar.activation(parts[:, s % 2, 0, c * CH:(c + 1) * CH], bank(n % 4), ACT.Identity,
                                     bias=qk_bias_sb[:, s % 2:s % 2 + 1]).then_inc(part1, 1)
                if n >= 1:
                    second_part(n - 1)
            second_part(2 * H * NCH - 1)

            def fill_v(g):
                nc.scalar.activation(view(v_slot, 0, [[HPG * HPG * D, B * H], [HPG * D + D, HPG], [1, D]]),
                                     view(work, g * (HPG * D), [[C, B * H], [D, HPG], [1, D]]),
                                     ACT.Copy).then_inc(v_slot_ready, 1)

            def exponentials(U, u):
                act.wait_ge(sub_done, U + 1)
                if not isinstance(U, int) or U >= ER:
                    act.wait_ge(pv_done, U - ER + 1)
                nc.scalar.activation(e_ring[:, u % ER, :], ps[:, 2 * (u % 2):2 * (u % 2) + 2, :], ACT.Exp
                                     ).then_inc(exp_done, 1)

            def inverse(U, u):
                act.wait_ge(sum_done, U + 1)
                nc.scalar.activation(s_ln[:, u % 2], s_sum[:, u % 2], ACT.Ln).then_inc(ln_done, 1)
                act.wait_ge(ln_done, U + 1)
                if not isinstance(U, int) or U >= 2:
                    act.wait_ge(norm_done, U - 1)
                nc.scalar.activation(s_inv[:, u % 2], s_ln[:, u % 2], ACT.Exp, scale=-1.0).then_inc(r_done, 1)

            def evacuate(g):
                act.wait_ge(pv_done, g * UPG)
                nc.scalar.activation(o_sb, bank(4), ACT.Copy).then_inc(acc_out, 1)

            def attention(g, first):
                for u in range(UPG):
                    U = g * UPG + u
                    if u == LAG and not first:
                        evacuate(g)
                        fill_v(g)
                    if u >= 1 or not first:
                        exponentials(U - 1, u - 1)
                    if u >= 2 or not first:
                        inverse(U - 2, u - 2)

            act.wait_ge(v_stored, TILES)
            act.wait_ge(pool_init, 2)
            act.wait_ge(part3, 2 * H * NCH)
            fill_v(0)
            attention(0, True)
            with act.Fori(1, NG) as g:
                attention(g, False)
            inverse(UNITS - 2, UPG - 2)
            exponentials(UNITS - 1, UPG - 1)
            inverse(UNITS - 1, UPG - 1)
            evacuate(NG)
            for c in range(NCH):
                deviation(2, c)
                normalise(2, c)

            def row_copy(j):
                act.wait_ge(rtr_done, j + 1)
                nc.scalar.activation(rows[:, 2 * j:2 * j + 2], ps[:, 5, :].rearrange("p (t c) -> p t c", t=2),
                                     ACT.Copy).then_inc(row_done, 1)

            for b in range(B + 1):
                if b < B:
                    act.wait_ge(tr2_done, b + 1)
                    nc.scalar.activation(xt[:, b % 2], bank(b % 2), ACT.Copy).then_inc(xt_done, 1)
                    act.wait_ge(xx_done, b + 1)
                    if b >= 2:
                        act.wait_ge(o_done, b - 1)
                    nc.scalar.activation(xxt[:, b % 2], bank(2), ACT.Copy).then_inc(xx_out, 1)
                if b >= 4:
                    row_copy(b - 4)
                if b >= 3 and b % 2 == 1:
                    deviation(3, (b - 3) // 2)
                    normalise(3, (b - 3) // 2)
            deviation(3, NCH - 1)
            normalise(3, NCH - 1)
            row_copy(B - 3)
            act.wait_ge(shifted, 1)
            nc.scalar.activation(s_view(COL + 4 * TILES, [1, TILES]), s_view(COL + 3 * TILES, [1, TILES]), ACT.Exp
                                 ).then_inc(gate_exp, 1)
            row_copy(B - 2)
            row_copy(B - 1)

            nc.scalar.preload_act_table(ACT.Gelu)

            def slot_step(s, r, body):
                if body(s):
                    act.wait_ge(xtr_done, s + 1)
                    if not isinstance(s, int) or s >= 2:
                        act.wait_ge(h_done, s - 1)
                    nc.scalar.activation(x_turned[:, r % 2], ps[:, 2 + r % 2, 0:C], ACT.Copy).then_inc(xt_out, 1)
                if body(s - 1):
                    act.wait_ge(h_done, s)
                    if not isinstance(s, int) or s >= 3:
                        act.wait_ge(gated_done, s - 2)
                    nc.scalar.activation(gelu1[:, (r + 1) % 2], ps[:, (r + 1) % 2, 0:C], ACT.Gelu).then_inc(gelu_done, 1)
                if body(s - 2):
                    act.wait_ge(gtr_done, s - 1)
                    if not isinstance(s, int) or s >= 4:
                        act.wait_ge(ye_done, s - 3)
                    nc.scalar.activation(gated_t[:, r % 2], ps[:, 4 + r % 2, 0:C], ACT.Copy).then_inc(gt_done, 1)

            slot_steps(act, slot_step)

        @block.vector
        def _(dve):
            chain = [0]

            def count(ins):
                chain[0] += 1
                ins.then_inc(dve_chain, 1)

            def link(*all_ins):
                for ins in all_ins:
                    count(ins)
                dve.wait_ge(dve_chain, chain[0])

            def statistics(k, c):
                for h in range(H):
                    for i in range(BPC):
                        b = c * BPC + i
                        count(nc.vector.bn_stats(stats[:, c, h * BPC + i], x_res[:, h, b * N:(b + 1) * N]))
                dve.wait_ge(dve_chain, chain[0])
                square, mean, scaled = (view(stats, c * SPC * 6 + i, [[6, SPC], [3, 2]]) for i in range(3))
                link(nc.vector.tensor_tensor(square, mean, mean, ALU.mult))
                nc.vector.scalar_tensor_tensor(out=square, in0=scaled, scalar=2.0 / N, in1=square, op0=ALU.mult,
                                               op1=ALU.add).then_inc(gn_sums[k], 1)

            def variance(k, c):
                dve.wait_ge(gn_group, NCH * k + c + 1)
                pg = view(ps, GN_BANK[k] * CH, [[2, SPC], [1, 2]])
                mean, var = gn[:, c, 0], gn[:, c, 1]
                link(nc.vector.tensor_copy(mean, pg[:, :, 1]))
                link(nc.vector.tensor_tensor(gn_tmp[:], mean, mean, ALU.mult))
                link(nc.vector.tensor_tensor(var, pg[:, :, 0], gn_tmp[:], ALU.subtract))
                nc.vector.tensor_scalar(var, var, 0.0, EPS, ALU.max, ALU.add).then_inc(gn_var, 1)

            def second_half(k, c):
                dve.wait_ge(gn_rstd, NCH * k + c + 1)
                mean, var, rstd = (gn[:, c, i] for i in range(3))
                link(nc.vector.scalar_tensor_tensor(out=gn_tmp[:], in0=rstd, scalar=-0.5, in1=rstd, op0=ALU.mult, op1=ALU.mult))
                link(nc.vector.tensor_tensor(gn_tmp[:], gn_tmp[:], var, ALU.mult))
                link(nc.vector.scalar_tensor_tensor(out=rstd, in0=gn_tmp[:], scalar=1.5, in1=rstd, op0=ALU.add, op1=ALU.mult))
                nc.vector.scalar_tensor_tensor(out=gn[:, c, 3], in0=mean, scalar=-1.0, in1=rstd, op0=ALU.mult,
                                               op1=ALU.mult).then_inc(gn_coef, 1)
                dve.wait_ge(gn_coef, NCH * k + c + 1)
                for i in range(BPC):
                    cols = slice((c * BPC + i) * N, (c * BPC + i + 1) * N)
                    nc.vector.tensor_scalar(x_hat[:, 1, cols], x_res[:, 1, cols], gn[:, c, 2, BPC + i:BPC + i + 1],
                                            gn[:, c, 3, BPC + i:BPC + i + 1], ALU.mult, ALU.add).then_inc(xhat_dve, 1)

            def unit_vectors(c):
                nc_cols = slice(c * CH, (c + 1) * CH)
                dve.wait_ge(n2_done, c + 1)
                nc.vector.tensor_scalar(rnorm, bank(c % 2), EPS_NORM2, None, ALU.max).then_inc(n2_floor, 1)
                dve.wait_ge(rn_done, c + 1)
                nc.vector.tensor_tensor(view(work, c * CH, [[T, H], [1, CH]]), x_hat[:, :, nc_cols],
                                        view(scratch, 0, [[0, H], [1, CH]]), ALU.mult).then_inc(fn_done, 1)
                dve.wait_ge(fn_done, c + 1)

            def correlations(d):
                dve.wait_ge(band_in[d], 16)
                if d == 0:
                    dve.wait_ge(conv_in, 16 * CONV)
                nc.vector.tensor_tensor(view(scratch, COR + d * TPC * NK, [[NK, TPC], [K, K], [1, K]]),
                                        view(scratch, BAND + d * TPC * WIN, [[WIN, TPC], [1, K], [SIDE, K]]),
                                        view(mask_sb, 0, [[0, TPC], [1, K], [0, K]]), ALU.mult).then_inc(cor_done, 1)

            def add_conv(d):
                dve.wait_ge(relu_done, H * (d + 1))
                xr = x_res[:, :, d * CH:(d + 1) * CH]
                nc.vector.tensor_tensor(xr, xr, view(scratch, YB, [[CH, H], [1, CH]]), ALU.add).then_inc(x1_done, 1)
                dve.wait_ge(x1_done, d + 1)

            dve.wait_ge(x_in[0], 16 * H)
            statistics(0, 0)
            variance(0, 0)
            second_half(0, 0)
            dve.wait_ge(x_in[1], 16 * H)
            statistics(0, 1)
            for t in range(NCH + 2):
                if t < NCH:
                    unit_vectors(t)
                if t + 1 < NCH:
                    variance(0, t + 1)
                    second_half(0, t + 1)
                if t + 2 < NCH:
                    dve.wait_ge(x_in[t + 2], 16 * H)
                    statistics(0, t + 2)
                if 0 <= t - 1 < NCH:
                    correlations(t - 1)
                if 0 <= t - 2:
                    variance(1, t - 2)
                    second_half(1, t - 2)
                if 0 <= t - 1 < NCH:
                    add_conv(t - 1)
                    statistics(1, t - 1)
            dve.wait_ge(consts_in, 16 * LATER)
            for n in range(2 * H * NCH):
                s, c = n // NCH, n % NCH
                dve.wait_ge(part1, n + 1)
                if n >= 2:
                    dve.wait_ge(part3, n - 1)
                nc.vector.scalar_tensor_tensor(out=rest[:, n % 2], in0=bank(n % 4), scalar=qk_bias_sb[:, s % 2:s % 2 + 1],
                                               in1=parts[:, s % 2, 0, c * CH:(c + 1) * CH], op0=ALU.add,
                                               op1=ALU.subtract).then_inc(rest_done, 1)
                dve.wait_ge(v_done, n + 1)
                nc.vector.tensor_tensor(v_all[:, n].rearrange("p (r d) -> p r d", d=D),
                                        ps[:, 6 + n % 2, 0:C].rearrange("p (r d) -> p r d", d=D),
                                        view(v_bias_sb, 0, [[0, HEADS], [1, D]]), ALU.add).then_inc(v_stored, 1)

            def maximum(U, u):
                dve.wait_ge(scores_done, U + 1)
                if not isinstance(U, int) or U >= 2:
                    dve.wait_ge(sub_done, U - 1)
                nc.vector.tensor_reduce(m_bf[:, u % 2], view(ps, 2 * (u % 2) * CH, [[1, P], [P, B]]), AX,
                                        ALU.max).then_inc(max_done, 1)

            def total(U, u):
                dve.wait_ge(exp_done, U + 1)
                if not isinstance(U, int) or U >= 2:
                    dve.wait_ge(r_done, U - 1)
                nc.vector.tensor_reduce(s_sum[:, u % 2], view(e_ring, (u % ER) * UW, [[1, P], [P, B]]), AX,
                                        ALU.add).then_inc(sum_done, 1)

            def add_heads(g, group):
                dve.wait_ge(acc_tr, group)
                xr = view(x_res, g * (HPG * D) - HPG * D, [[T, H], [N, B], [1, HPG * D]])
                nc.vector.tensor_tensor(xr, xr, view(ps, 5 * CH, [[N, H], [HPG * D, B], [1, HPG * D]]),
                                        ALU.add).then_inc(x2_added, 1)

            def attention(g, first):
                for u in range(UPG):
                    U = g * UPG + u
                    maximum(U, u)
                    if u >= 1 or not first:
                        total(U - 1, u - 1)
                    if u == LAG + 2 and not first:
                        add_heads(g, g)

            attention(0, True)
            with dve.Fori(1, NG) as g:
                attention(g, False)
            total(UNITS - 1, UPG - 1)
            add_heads(NG, NG)

            dve.wait_ge(x2_added, NG)
            for c in range(NCH):
                statistics(2, c)
                if c >= 1:
                    variance(2, c - 1)
                    second_half(2, c - 1)
            variance(2, NCH - 1)
            second_half(2, NCH - 1)
            def choose(c):
                def per_token(i):
                    return s_view(i * TILES * E + c * TPC * E, [E, TPC], [1, E])

                def column(i):
                    return s_view(COL + i * TILES + c * TPC, [1, TPC], [0, E])

                def best(logit, top, hot):
                    col, first = (s_view(COL + i * TILES + c * TPC, [1, TPC]) for i in (top, 2))
                    link(nc.vector.tensor_reduce(col, per_token(logit), AX, ALU.max))
                    link(nc.vector.tensor_tensor(per_token(3), per_token(logit), column(top), ALU.is_equal))
                    link(nc.vector.tensor_tensor(per_token(3), per_token(3), view(rank_sb, 0, [[0, TPC], [1, E]]), ALU.mult))
                    link(nc.vector.tensor_reduce(first, per_token(3), AX, ALU.max))
                    link(nc.vector.tensor_tensor(per_token(hot), per_token(3), column(2), ALU.is_equal))

                dve.wait_ge(logits_done, c + 1)
                nc.vector.tensor_copy(per_token(0), ps[:, 6, c * TPC * E:(c + 1) * TPC * E].rearrange("p (t e) -> p t e", e=E)
                                      ).then_inc(logits_read, 1)
                dve.wait_ge(logits_read, c + 1)
                best(0, 0, 4)
                link(nc.vector.scalar_tensor_tensor(out=per_token(1), in0=per_token(4), scalar=-HUGE, in1=per_token(0),
                                                    op0=ALU.mult, op1=ALU.add))
                best(1, 1, 5)
                nc.vector.tensor_tensor(mask_bf[:, c * TPC:(c + 1) * TPC], per_token(4), per_token(5), ALU.add
                                        ).then_inc(mask_done, 1)

            for b in range(B + 1):
                if b < B:
                    dve.wait_ge(cx_done, b + 1)
                    if b >= 2:
                        dve.wait_ge(o_done, b - 1)
                    nc.vector.tensor_copy(cx[:, b % 2], ps[:, 3, :].rearrange("p (n c) -> p n c", n=2)).then_inc(cx_out, 1)
                if b >= 1:
                    dve.wait_ge(o_done, b)
                    dve.wait_ge(xsum_done, b)
                    xr = x_res[:, :, (b - 1) * N:b * N]
                    nc.vector.scalar_tensor_tensor(out=xr, in0=ps[:, 4, :].rearrange("p (h n) -> p h n", h=H),
                                                   scalar=gamma_sb[:, 0:1], in1=xr, op0=ALU.mult, op1=ALU.add
                                                   ).then_inc(x3_done, 1)
                if b >= 2 and b % 2 == 0:
                    dve.wait_ge(x3_done, b)
                    statistics(3, (b - 2) // 2)
                if b >= 3 and b % 2 == 1:
                    variance(3, (b - 3) // 2)
                    second_half(3, (b - 3) // 2)
                    if b >= 5:
                        choose((b - 5) // 2)
            variance(3, NCH - 1)
            second_half(3, NCH - 1)

            choose(2)
            choose(3)

            def col(i):
                return s_view(COL + i * TILES, [1, TILES])

            def per_token(i):
                return s_view(i * TILES * E, [E, TILES], [1, E])

            def column(i):
                return s_view(COL + i * TILES, [1, TILES], [0, E])

            def starts(buf, back, *dims):
                return s_view(START + buf * 2 * E + E - back, *(dims or ([1, E],)))

            nc.vector.tensor_tensor(col(3), col(1), col(0), ALU.subtract).then_inc(shifted, 1)
            count(nc.vector.memset(starts(0, E, [1, 4 * E]), 0.0))
            dve.wait_ge(ranks_done, NCH)
            link(nc.vector.tensor_scalar(s_view(TILE_N, [1, E]), ps[:, 7, RANK + TILES * E:RANK + (TILES + 1) * E],
                                         1.0 / P, (P - 1) / (2.0 * P), ALU.mult, ALU.add))
            dve.wait_ge(gate_exp, 1)
            link(nc.vector.tensor_scalar(s_view(TILE_N, [1, E]), s_view(TILE_N, [1, E]), ROUND, None, ALU.add),
                 nc.vector.tensor_scalar(col(5), col(4), 1.0, None, ALU.add))
            link(nc.vector.tensor_scalar(starts(0, 0), s_view(TILE_N, [1, E]), ROUND, None, ALU.subtract),
                 nc.vector.reciprocal(col(6), col(5)))
            link(nc.vector.tensor_tensor(starts(1, 0), starts(0, 0), starts(0, 1), ALU.add),
                 nc.vector.tensor_tensor(col(7), col(4), col(6), ALU.mult))
            link(nc.vector.tensor_tensor(starts(0, 0), starts(1, 0), starts(1, 2), ALU.add),
                 nc.vector.tensor_tensor(per_token(6), per_token(4), column(6), ALU.mult))
            link(nc.vector.tensor_tensor(starts(1, 0), starts(0, 0), starts(0, 4), ALU.add),
                 nc.vector.tensor_tensor(per_token(7), per_token(5), column(7), ALU.mult))
            link(nc.vector.scalar_tensor_tensor(out=per_token(8), in0=starts(1, 1, [0, TILES], [1, E]), scalar=float(P),
                                                in1=ps[:, 7, RANK:RANK + TILES * E].rearrange("p (t e) -> p t e", e=E),
                                                op0=ALU.mult, op1=ALU.add))
            nc.vector.tensor_tensor(per_token(7), per_token(6), per_token(7), ALU.add).then_inc(comb_done, 1)
            link(nc.vector.tensor_tensor(s_view(9 * TILES * E, [TILES * E, TOP], [1, TILES * E]),
                                         s_view(4 * TILES * E, [TILES * E, TOP], [1, TILES * E]),
                                         s_view(8 * TILES * E, [0, TOP], [1, TILES * E]), ALU.mult))
            pos, hi, lo = (s_view(o, [1, PAIRS]) for o in (POS, HI, LO))
            link(nc.vector.tensor_reduce(pos, s_view(9 * TILES * E, [E, PAIRS], [1, E]), AX, ALU.add))
            link(nc.vector.tensor_scalar(hi, pos, 1.0 / P, -(P - 1) / (2.0 * P), ALU.mult, ALU.add))
            link(nc.vector.tensor_scalar(hi, hi, ROUND, None, ALU.add))
            link(nc.vector.tensor_scalar(hi, hi, ROUND, None, ALU.subtract))
            nc.vector.scalar_tensor_tensor(out=lo, in0=hi, scalar=-float(P), in1=pos, op0=ALU.mult, op1=ALU.add
                                           ).then_inc(places_done, 1)
            nc.vector.tensor_tensor(hot_hi[:, 2], view(tab, KNUM, [[0, PAIRS], [1, SLOTS]]),
                                    s_view(HI, [1, PAIRS], [0, SLOTS]), ALU.is_equal).then_inc(tiles_hot, 1)
            dve.wait_ge(tiles_hot, 1)
            nc.vector.tensor_scalar(hot_hi[:, 1], hot_hi[:, 2], tab[:, PLACE:PLACE + 1], None, ALU.mult).then_inc(hots_done, 1)
            dve.wait_ge(places_done, 1)
            for q in range(4):
                n = PAIRS // 4
                nc.vector.tensor_tensor(hot_lo[:, q * n:(q + 1) * n], view(tab, NUM, [[0, n], [1, P]]),
                                        s_view(LO + q * n, [1, n], [0, P]), ALU.is_equal).then_inc(hots_done, 1)
            link(nc.vector.tensor_tensor(s_view(OWN, [E, SLOTS], [1, E]), view(tab, KNUM, [[1, SLOTS], [0, E]]),
                                         starts(1, 0, [0, SLOTS], [1, E]), ALU.is_ge))
            link(nc.vector.tensor_reduce(s_view(EXPERT, [1, SLOTS]), s_view(OWN, [E, SLOTS], [1, E]), AX, ALU.add))
            link(nc.vector.tensor_scalar(s_view(EXPERT, [1, SLOTS]), s_view(EXPERT, [1, SLOTS]), float(E - 1), None, ALU.min))
            link(nc.vector.tensor_copy(slot_e[:, 0:SLOTS], s_view(EXPERT, [1, SLOTS])),
                 nc.vector.tensor_tensor(s_view(OWN, [E, SLOTS], [1, E]), view(tab, NUM, [[0, SLOTS], [1, E]]),
                                         s_view(EXPERT, [1, SLOTS], [0, E]), ALU.is_equal))
            dve.wait_ge(slots_done, 1)
            of_tile, in_tile, empty = ps[:, 4, 0:SLOTS], ps[:, 4, SLOTS:2 * SLOTS], s_view(EMPTY, [1, SLOTS])
            link(nc.vector.tensor_scalar(empty, in_tile, 0.0, tab[:, PAD:PAD + 1], ALU.is_equal, ALU.mult))
            link(nc.vector.tensor_tensor(empty, empty, of_tile, ALU.add))
            nc.vector.scalar_tensor_tensor(out=slot_x[:], in0=in_tile, scalar=-1.0, in1=empty, op0=ALU.add, op1=ALU.add
                                           ).then_inc(plan_done, 1)

            def slot_step(s, r, body):
                if body(s):
                    dve.wait_ge(xr_in[r], (s - r) * (16 // XR) + 16)
                    if not isinstance(s, int) or s >= 1:
                        dve.wait_ge(gate_done, s)
                    nc.vector.tensor_tensor(s_view(OWN_GATE, [1, E]), x_rows[:, r, C:C + E],
                                            view(scratch, s * E + OWN, [[1, E]]), ALU.mult).then_inc(gate_own, 1)
                    dve.wait_ge(gate_own, s + 1)
                    nc.vector.tensor_reduce(view(scratch, s + GATE, [[1, 1]]), s_view(OWN_GATE, [1, E]), AX, ALU.add
                                            ).then_inc(gate_done, 1)
                if body(s - 1):
                    dve.wait_ge(gelu_done, s)
                    if not isinstance(s, int) or s >= 3:
                        dve.wait_ge(gtr_done, s - 2)
                    nc.vector.tensor_tensor(gated[:, (r + 1) % 2], ps[:, (r + 1) % 2, C:2 * C], gelu1[:, (r + 1) % 2],
                                            ALU.mult).then_inc(gated_done, 1)
                if body(s - 3):
                    dve.wait_ge(ye_done, s - 2)
                    if not isinstance(s, int) or s >= 7:
                        dve.wait_ge(y_out, (s - 6) * 16)
                    nc.vector.tensor_scalar(y_rows[:, (r + 1) % 4], ps[:, 6 + (r + 1) % 2, 0:C],
                                            view(scratch, (s - 3) + GATE, [[1, 1]]), None, ALU.mult).then_inc(ye_out, 1)

            slot_steps(dve, slot_step)
            for c in range(NCH):
                for b in range(c * BPC, (c + 1) * BPC):
                    dve.wait_ge(ytr_done, b + 1)
                    xr = x_res[:, :, b * N:(b + 1) * N]
                    nc.vector.tensor_tensor(xr, xr, ps[:, b % 2, :].rearrange("p (h n) -> p h n", h=H), ALU.add
                                            ).then_inc(x4_done, 1)

        @block.tensor
        def _(pe):
            def group_norm(k, c):
                q = NCH * k + c
                pe.wait_ge(gn_sums[k], c + 1)
                if q >= 1:
                    pe.wait_ge(gn_var, q)
                for i in range(2):
                    last = nc.tensor.matmul(view(ps, GN_BANK[k] * CH, [[2, SPC], [1, 2]]), group_sb[:],
                                            stats[:, c, :, 3 * i:3 * i + 2], start=(i == 0), stop=(i == 1))
                last.then_inc(gn_group, 1)

            def normed(k, b):
                pe.wait_ge(xhat_act, B * k + b + 1)
                pe.wait_ge(xhat_dve, B * k + b + 1)

            pe.wait_ge(first_in, 16 * FIRST)
            def norms(c):
                pe.wait_ge(sq_done, c + 1)
                if c >= 2:
                    pe.wait_ge(n2_floor, c - 1)
                for h in range(H):
                    last = nc.tensor.matmul(bank(c % 2), ones_sb[:], work[:, h * T + c * CH:h * T + (c + 1) * CH],
                                            start=(h == 0), stop=(h == H - 1))
                last.then_inc(n2_done, 1)

            def gram(c):
                pe.wait_ge(fn_done, c + 1)
                for t in range(TPC):
                    i, hb = c * TPC + t, t % 2
                    if i >= 2:
                        pe.wait_ge(gram_row, i - 1)
                    q0 = (i // 2) * N + (P - REACH if hb else 0)
                    for h in range(H):
                        last = nc.tensor.matmul(ps[:, 2 + i % 2, 0:ROW - REACH], work[:, h * T + i * P:h * T + (i + 1) * P],
                                                work[:, h * T + q0:h * T + q0 + ROW - REACH],
                                                start=(h == 0), stop=(h == H - 1))
                    last.then_inc(gram_done, 1)

            def conv_features(d):
                if d == 0:
                    pe.wait_ge(conv_in, 16 * CONV)
                for o in range(H):
                    if d >= 1:
                        pe.wait_ge(relu_done, H * (d - 1) + o + 1)
                    for h in range(H):
                        nc.tensor.matmul(bank(6 + o), conv_wT_sb[:, h, o * P:(o + 1) * P],
                                         x_hat[:, h, d * CH:(d + 1) * CH], start=(h == 0), stop=False)

            def turn_correlations(d):
                pe.wait_ge(cor_done, d + 1)
                if d >= 1:
                    pe.wait_ge(cor_t_done, d)
                for t in range(TPC):
                    last = nc.tensor.transpose(ps[0:NK, 4, t * P:(t + 1) * P],
                                               view(scratch, COR + (d * TPC + t) * NK, [[1, NK]]), ident[:])
                last.then_inc(cor_tr, 1)

            def conv_correlations(d):
                pe.wait_ge(cor_t_done, d + 1)
                for o in range(H):
                    nc.tensor.matmul(bank(6 + o), conv_cT_sb[:, o * P:(o + 1) * P], cor_t[:, d * CH:(d + 1) * CH],
                                     start=False, stop=True).then_inc(y_done, 1)

            group_norm(0, 0)
            for t in range(NCH + 2):
                if t < NCH:
                    norms(t)
                if t + 1 < NCH:
                    group_norm(0, t + 1)
                if 0 <= t - 1 < NCH:
                    conv_features(t - 1)
                if t < NCH:
                    gram(t)
                if 0 <= t - 1 < NCH:
                    turn_correlations(t - 1)
                if 0 <= t - 2:
                    group_norm(1, t - 2)
                if 0 <= t - 1 < NCH:
                    conv_correlations(t - 1)
            pe.wait_ge(consts_in, 16 * LATER)
            for n in range(2 * H * NCH):
                s, c = n // NCH, n % NCH
                h = s // 2
                normed(1, BPC * (c + 1) - 1)
                if n >= 4:
                    pe.wait_ge(rest_done, n - 3)
                nc.tensor.matmul(bank(n % 4), qkv_sb[:, s % 2], x_hat[:, h, c * CH:(c + 1) * CH],
                                 start=True, stop=True).then_inc(qk_done, 1)
                normed(1, n // 2)
                if n >= 2:
                    pe.wait_ge(v_stored, n - 1)
                for h in range(H):
                    last = nc.tensor.matmul(ps[:, 6 + n % 2, h * P:(h + 1) * P], x_hat[:, h, n * P:(n + 1) * P],
                                            qkv_sb[:, 2], start=True, stop=True)
                last.then_inc(v_done, 1)

            def scores(U, u, g):
                i, mh, nh = u // 4, (u // 2) % 2, u % 2
                if u % 4 == 0:
                    pe.wait_ge(stack_in[i], (g + 1) * (2 * PARTS * 16))
                if not isinstance(U, int) or U >= 2:
                    pe.wait_ge(exp_done, U - 1)
                for b in range(B):
                    last = nc.tensor.matmul(ps[:, 2 * (u % 2) + b // 4, (b % 4) * P:(b % 4 + 1) * P],
                                            k_stack[:, i, b * N + mh * P:b * N + (mh + 1) * P],
                                            q_stack[:, i, b * N + nh * P:b * N + (nh + 1) * P],
                                            start=(b % 4 == 0), stop=(b % 4 == 3), skip_group_check=True)
                last.then_inc(scores_done, 1)

            def subtract(U, u):
                pe.wait_ge(max_done, U + 1)
                for j in range(2):
                    last = nc.tensor.matmul(bank(2 * (u % 2) + j), ident_neg[:],
                                            view(m_bf, (u % 2) * P, [[0, B // 2], [1, P]]), start=False, stop=True,
                                            skip_group_check=True)
                last.then_inc(sub_done, 1)

            def product(U, u, g):
                i, mh, nh = u // 4, (u // 2) % 2, u % 2
                if u == 0:
                    pe.wait_ge(v_slot_ready, g + 1)
                pe.wait_ge(norm_done, U + 1)
                for b in range(B):
                    last = nc.tensor.matmul(ps[32 * (b % 4):32 * (b % 4) + 32, 4, (b // 4) * N + nh * P:(b // 4) * N + (nh + 1) * P],
                                            v_slot[:, b * H + mh, i, :], e_ring[:, u % ER, b * P:(b + 1) * P],
                                            start=(u == 0 and b < 4), stop=(u == UPG - 1), skip_group_check=True)
                last.then_inc(pv_done, 1)

            def transpose_heads(group):
                pe.wait_ge(acc_out, group)
                if not isinstance(group, int) or group >= 2:
                    pe.wait_ge(x2_added, group - 1)
                for nh in range(H):
                    for j in range(2):
                        last = nc.tensor.transpose(ps[:, 5, (2 * nh + j) * P:(2 * nh + j + 1) * P],
                                                   o_sb[:, j * N + nh * P:j * N + (nh + 1) * P], ident[:])
                last.then_inc(acc_tr, 1)

            def attention(g, first):
                for u in range(UPG):
                    U = g * UPG + u
                    scores(U, u, g)
                    if u >= 1 or not first:
                        subtract(U - 1, (u - 1) % UPG)
                    if u >= LAG:
                        product(U - LAG, u - LAG, g)
                    elif not first:
                        product(U - LAG, u - LAG + UPG, g)
                    if u == LAG + 1 and not first:
                        transpose_heads(g)

            pe.wait_ge(rest_done, 2 * H * NCH)
            attention(0, True)
            with pe.Fori(1, NG) as g:
                attention(g, False)
            subtract(UNITS - 1, UPG - 1)
            for u in range(UPG - LAG, UPG):
                product((NG - 1) * UPG + u, u, NG - 1)
            transpose_heads(NG)

            for c in range(NCH):
                group_norm(2, c)

            def logits(c):
                normed(3, BPC * (c + 1) - 1)
                if c >= 1:
                    pe.wait_ge(logits_read, c)
                for t in range(c * TPC, (c + 1) * TPC):
                    for h in range(H):
                        last = nc.tensor.matmul(ps[:, 6, t * E:(t + 1) * E], x_hat[:, h, t * P:(t + 1) * P], gate_sb[:, h],
                                                start=(h == 0), stop=(h == H - 1))
                last.then_inc(logits_done, 1)

            def token_rows(b):
                normed(3, b)
                if b >= 1:
                    pe.wait_ge(row_done, b)
                for t in range(2):
                    for h in range(H):
                        last = nc.tensor.transpose(ps[:, 5, t * C + h * P:t * C + (h + 1) * P],
                                                   x_hat[:, h, (2 * b + t) * P:(2 * b + t + 1) * P], ident[:])
                last.then_inc(rtr_done, 1)

            def ranks(c):
                pe.wait_ge(mask_done, c + 1)
                if c == 0:
                    pe.wait_ge(gn_var, 4 * NCH)
                for t in range(c * TPC, (c + 1) * TPC):
                    nc.tensor.matmul(ps[:, 7, RANK + t * E:RANK + (t + 1) * E], before_bf[:], mask_bf[:, t],
                                     start=(t == 0), stop=True, skip_group_check=True)
                    last = nc.tensor.matmul(view(ps, 7 * CH + RANK + (t + 1) * E, [[E, TILES - t], [1, E]]), ones_bf[:],
                                            view(mask_bf, t * E, [[0, TILES - t], [1, E]]), start=False, stop=True,
                                            skip_group_check=True)
                last.then_inc(ranks_done, 1)

            for b in range(B + 1):
                if b < B:
                    normed(2, b)
                    if b >= 2:
                        pe.wait_ge(xt_done, b - 1)
                    for nh in range(2):
                        for h in range(H):
                            last = nc.tensor.transpose(ps[:, b % 2, nh * C + h * P:nh * C + (h + 1) * P],
                                                       x_hat[:, h, b * N + nh * P:b * N + (nh + 1) * P], ident[:])
                    last.then_inc(tr2_done, 1)
                    if b >= 1:
                        pe.wait_ge(cx_out, b)
                    for o in range(H):
                        for h in range(H):
                            last = nc.tensor.matmul(ps[:, 3, o * N:(o + 1) * N], gram_wT_sb[:, h, o * P:(o + 1) * P],
                                                    x_hat[:, h, b * N:(b + 1) * N], start=(h == 0), stop=(h == H - 1))
                    last.then_inc(cx_done, 1)
                if b >= 1:
                    a = b - 1
                    pe.wait_ge(xx_out, a + 1)
                    pe.wait_ge(cx_out, a + 1)
                    if a >= 1:
                        pe.wait_ge(x3_done, a)
                    for o in range(H):
                        for h in range(H):
                            last = nc.tensor.matmul(ps[:, 4, o * N:(o + 1) * N], xxt[:, a % 2, h, o * P:(o + 1) * P],
                                                    cx[:, a % 2, h, :], start=(h == 0), stop=(h == H - 1))
                    last.then_inc(o_done, 1)
                if b < B:
                    pe.wait_ge(xt_done, b + 1)
                    if b >= 1:
                        pe.wait_ge(xx_out, b)
                    for o in range(H):
                        for n in range(2):
                            last = nc.tensor.matmul(ps[:, 2, o * C:(o + 1) * C], xt[:, b % 2, n, o * P:(o + 1) * P],
                                                    xt[:, b % 2, n, :], start=(n == 0), stop=(n == 1))
                    last.then_inc(xx_done, 1)

                if b >= 2 and b % 2 == 0:
                    group_norm(3, (b - 2) // 2)
                if b >= 4:
                    if b % 2 == 0:
                        logits((b - 4) // 2)
                    token_rows(b - 4)
            ranks(0)
            ranks(1)
            logits(NCH - 1)
            token_rows(B - 3)
            ranks(2)
            ranks(3)
            token_rows(B - 2)
            token_rows(B - 1)
            pe.wait_ge(tiles_scaled, 1)
            for q in range(4):
                pe.wait_ge(hots_done, q + 2)
                for j in range(q * PAIRS // 4, (q + 1) * PAIRS // 4):
                    last = nc.tensor.matmul(ps[:, 4, 0:2 * SLOTS], hot_lo[:, j], hot_hi[:, 0:2, j],
                                            start=(j == 0), stop=(j == PAIRS - 1))
            last.then_inc(slots_done, 1)
            pe.wait_ge(w_in, 64)
            pe.wait_ge(plan_done, 1)

            def slot_step(s, r, body):
                if body(s):
                    pe.wait_ge(xr_in[r], (s - r) * (16 // XR) + 16)
                    if not isinstance(s, int) or s >= 2:
                        pe.wait_ge(xt_out, s - 1)
                    for h in range(H):
                        last = nc.tensor.transpose(ps[:, 2 + r % 2, h * P:(h + 1) * P], x_rows[:, r, h * P:(h + 1) * P], ident[:])
                    last.then_inc(xtr_done, 1)
                if body(s - 1):
                    e = pe.value_load(slot_e[0:1, bass.ds(s - 1, 1)], min_val=0, max_val=E - 1)
                    pe.wait_ge(xt_out, s)
                    if not isinstance(s, int) or s >= 3:
                        pe.wait_ge(gated_done, s - 2)
                    for h in range(H):
                        last = nc.tensor.matmul(bank((r + 1) % 2), x_turned[:, (r + 1) % 2, h * P:(h + 1) * P],
                                                w13_sb[:, h, bass.ds(e * (2 * C), 2 * C)], start=(h == 0), stop=(h == H - 1))
                    last.then_inc(h_done, 1)
                if body(s - 2):
                    pe.wait_ge(gated_done, s - 1)
                    if not isinstance(s, int) or s >= 4:
                        pe.wait_ge(gt_done, s - 3)
                    for f in range(2):
                        last = nc.tensor.transpose(ps[:, 4 + r % 2, f * P:(f + 1) * P], gated[:, r % 2, f * P:(f + 1) * P], ident[:])
                    last.then_inc(gtr_done, 1)
                if body(s - 3):
                    e = pe.value_load(slot_e[0:1, bass.ds(s - 3, 1)], min_val=0, max_val=E - 1)
                    pe.wait_ge(gt_done, s - 2)
                    if not isinstance(s, int) or s >= 5:
                        pe.wait_ge(ye_out, s - 4)
                    for f in range(2):
                        last = nc.tensor.matmul(ps[:, 6 + (r + 1) % 2, 0:C], gated_t[:, (r + 1) % 2, f * P:(f + 1) * P],
                                                w2_sb[:, f, bass.ds(e * C, C)], start=(f == 0), stop=(f == 1))
                    last.then_inc(ye_done, 1)

            slot_steps(pe, slot_step)
            for b in range(B):
                pe.wait_ge(y_in[b // BPC], 16)
                if b >= 2:
                    pe.wait_ge(x4_done, b - 1)
                for h in range(H):
                    for nh in range(2):
                        last = nc.tensor.transpose(ps[:, b % 2, h * N + nh * P:h * N + (nh + 1) * P],
                                                   y_back[:, 2 * b + nh, h * P:(h + 1) * P], ident[:])
                last.then_inc(ytr_done, 1)


def _arrays(x, L0_conv_conv_w, L0_conv_conv_b, L1_conv_w_qkv, L1_conv_b_qkv, L2_conv_W, L2_conv_gamma,
            L3_conv_gate_w, L3_conv_w1, L3_conv_w2, L3_conv_w3):
    import numpy as np
    f = np.float32
    C, P, D, S, K = 256, 128, 8, 16, 5
    E = L3_conv_w1.shape[0]
    conv_w = np.asarray(L0_conv_conv_w)
    w_qkv, b_qkv = np.asarray(L1_conv_w_qkv), np.asarray(L1_conv_b_qkv)
    blocks = np.zeros((3, P, P), f)
    for s in range(3):
        for r in range(P // D):
            blocks[s, r * D:(r + 1) * D, r * D:(r + 1) * D] = w_qkv[s * D:(s + 1) * D].T
    w13T = np.stack([np.asarray(L3_conv_w1), np.asarray(L3_conv_w3)], 1)
    col = np.arange(P) % S
    shift = np.arange(K) - K // 2
    inside = (col[:, None] + shift[None] >= 0) & (col[:, None] + shift[None] < S)
    group = np.arange(P) // 8
    TILES, T = 16, 2048
    SLOTS = (2 * T + E * (P - 1)) // P
    place = np.arange(P)[:, None]
    tables = np.concatenate([np.broadcast_to(np.arange(P), (P, P)), np.broadcast_to(np.arange(SLOTS), (P, SLOTS)),
                             np.broadcast_to(np.tile(np.arange(TILES) * P, 2), (P, 2 * TILES)), place + 1, T + 1 + place], 1)
    return {
        "x": np.asarray(x),
        "conv_wT": conv_w[:, :C].T.reshape(2, P, C),
        "conv_cT": conv_w[:, C:].T,
        "conv_b": np.asarray(L0_conv_conv_b).reshape(2, P).T,
        "qkv_blocks": blocks,
        "qk_bias": np.stack([np.tile(b_qkv[:D], P // D), np.tile(b_qkv[D:2 * D], P // D)], 1),
        "v_bias": np.broadcast_to(b_qkv[2 * D:], (P, D)),
        "gram_wT": np.asarray(L2_conv_W).T.reshape(2, P, C),
        "gamma": np.broadcast_to(np.asarray(L2_conv_gamma).reshape(1, 1), (P, 1)),
        "gate_wT": np.asarray(L3_conv_gate_w).T,
        "w13T": w13T.transpose(3, 0, 1, 2).reshape(2, P, E * 2 * C),
        "w2T": np.asarray(L3_conv_w2).transpose(2, 0, 1).reshape(2, P, E * C),
        "identity": np.eye(P, dtype=f),
        "ones": np.ones((P, P), f),
        "group_ones": (group[:, None] == group[None]).astype(f) / f(16),
        "edge_mask": inside.astype(f),
        "expert_rank": np.broadcast_to(np.arange(E, 0, -1).astype(f), (P, E)),
        "before": (np.arange(P)[:, None] < np.arange(P)[None]).astype(f),
        "tables": tables.astype(f),
    }


def kernel(**inputs):
    import numpy as _np
    import concourse.bacc as _bacc
    from concourse import mybir as _mybir
    from concourse.bass_utils import run_bass_kernel_spmd as _run

    nc = _bacc.Bacc("TRN2", target_bir_lowering=False, num_devices=1)
    arrays, args = {}, []
    for name, a in _arrays(**inputs).items():
        a = _np.ascontiguousarray(a)
        arrays[f"in_{name}_dram"] = a
        args.append(nc.dram_tensor(f"in_{name}_dram", a.shape, _mybir.dt.from_np(a.dtype), kind="ExternalInput").ap())
    shape = tuple(inputs["x"].shape)
    args.append(nc.dram_tensor("out_0_dram", shape, _mybir.dt.float32, kind="ExternalOutput").ap())
    conv_stack_kernel(nc, *args)
    r = _run(nc, [arrays], core_ids=[0])
    return r.results[0]["out_0_dram"]
```

```python
import concourse.bass as bass
from concourse import mybir
from contextlib import ExitStack


def conv_stack_kernel(nc, x, conv_wT, conv_cT, conv_b, qkv_blocks, qk_bias, v_bias, gram_wT, gamma,
                      gate_wT, w13T, w2T, identity, ones, group_ones, edge_mask, expert_rank,
                      before, tables,
                      out):
    fp32, bf16 = mybir.dt.float32, mybir.dt.bfloat16
    ALU, ACT, AX = mybir.AluOpType, mybir.ActivationFunctionType, mybir.AxisListType.X

    B, C, SIDE = x.shape[0], x.shape[1], x.shape[2]
    N = SIDE * SIDE
    P = 128
    H = C // P
    T = B * N
    TILES = T // P
    CH = 512
    NCH = T // CH
    BPC = CH // N
    K = 5
    NK = K * K
    REACH = (K // 2) * (SIDE + 1)
    WIN = 2 * REACH + 1
    ROW = P + 2 * REACH
    HEADS, D = 32, C // 32
    PARTS = 3
    KR = PARTS * PARTS * D
    HPG = 4
    NG = HEADS // HPG
    UPG = HPG * 4
    UNITS = NG * UPG
    UW = B * P
    ER = 8
    LAG = 6
    POOLED = 116
    POOLED_LAST = 56
    E = gate_wT.shape[1]
    TOP = 2
    PAIRS = TOP * TILES
    SLOTS = (TOP * T + E * (P - 1)) // P
    YROWS = T + P
    EPS = 1e-5
    ROUND = 1.5 * 2.0 ** 23
    EPS_NORM2 = 1e-24

    gram_dram = nc.dram_tensor("gram_rows", (TILES, P, ROW), fp32, kind="Internal").ap()
    part_dram = nc.dram_tensor("qk_parts", (2, PARTS, C, T), bf16, kind="Internal").ap()
    row_dram = nc.dram_tensor("token_rows", (YROWS, C + E), fp32, kind="Internal").ap()
    y_dram = nc.dram_tensor("expert_sums", (YROWS, C), fp32, kind="Internal").ap()

    ctx = ExitStack()
    with ctx:
        def sb(name, shape, dt=fp32):
            return ctx.enter_context(nc.sbuf_tensor(name, shape, dt))

        def sem(name):
            return ctx.enter_context(nc.semaphore(name))

        def view(t, off, dims, rows=P):
            width = 1
            for s in t.shape[1:]:
                width *= s
            return bass.AP(t, off, [[width, rows]] + [list(d) for d in dims])

        x_res = sb("x_res", [P, H, T])
        x_hat = sb("x_hat", [P, H, T])
        work = sb("work", [P, H * T])
        e_ring = sb("e_ring", [P, ER, UW])
        scratch = sb("scratch", [P, 6144])
        q_stack = sb("q_stack", [KR, HPG, T], bf16)
        k_stack = sb("k_stack", [KR, HPG, T], bf16)
        v_slot = sb("v_slot", [P, B * H, HPG, HPG * D])
        w13_sb = sb("w13_sb", [P, H, E * 2 * C])
        w2_sb = sb("w2_sb", [P, H, E * C])
        conv_wT_sb = sb("conv_wT_sb", [P, H, C])
        conv_cT_sb = sb("conv_cT_sb", [NK, C])
        conv_b_sb = sb("conv_b_sb", [P, H])
        qkv_sb = sb("qkv_sb", [P, 3, P])
        qk_bias_sb = sb("qk_bias_sb", [P, 2])
        v_bias_sb = sb("v_bias_sb", [P, D])
        gram_wT_sb = sb("gram_wT_sb", [P, H, C])
        gamma_sb = sb("gamma_sb", [P, 1])
        gate_sb = sb("gate_sb", [P, H, E])
        ident = sb("ident", [P, P])
        ident_neg = sb("ident_neg", [P, P], bf16)
        ones_sb = sb("ones_sb", [P, P])
        group_sb = sb("group_sb", [P, P])
        mask_sb = sb("mask_sb", [P, K])
        rank_sb = sb("rank_sb", [P, E])
        before_sb = sb("before_sb", [P, P])
        before_bf = sb("before_bf", [P, P], bf16)
        ones_bf = sb("ones_bf", [P, P], bf16)
        mask_bf = sb("mask_bf", [P, TILES, E], bf16)
        NUM, KNUM, TILE0, PLACE, PAD = 0, P, P + SLOTS, P + SLOTS + PAIRS, P + SLOTS + PAIRS + 1
        tab = sb("tab", [P, PAD + 1])
        slot_x = sb("slot_x", [P, SLOTS], mybir.dt.uint32)
        slot_e = sb("slot_e", [P, SLOTS + 1], mybir.dt.int32)
        SPC = H * BPC
        stats = sb("stats", [P, NCH, SPC, 6])
        gn = sb("gn", [P, NCH, 4, SPC])
        gn_tmp = sb("gn_tmp", [P, SPC])
        m_bf = sb("m_bf", [P, 2, P], bf16)
        s_ln = sb("s_ln", [P, 2, P])
        s_inv = sb("s_inv", [P, 2, P])
        ps = ctx.enter_context(nc.psum_tensor("ps", [P, 8, CH], fp32))

        TPC = CH // P
        rnorm = scratch[:, 0:CH]
        GST = CH
        BAND = GST + 2 * TPC * ROW
        COR = BAND + TILES * WIN
        YB = COR + TILES * NK
        cor_t = view(e_ring, 0, [[1, T]], rows=NK)
        o_sb = scratch[:, 0:CH]
        parts = scratch[:, :].bitcast(bf16).rearrange("p (s a t) -> p s a t", s=2, a=PARTS)
        score_bf = x_hat[:, 0, 3 * CH:4 * CH].bitcast(bf16).rearrange("p (s n) -> p s n", s=2)
        max4 = x_hat[:, 1, 0:2 * P].bitcast(bf16)
        max2 = x_hat[:, 1, 2 * P:3 * P].bitcast(bf16)
        sum4 = x_hat[:, 0, 0:2 * CH].rearrange("p (s n) -> p s n", s=2)
        sum2 = x_hat[:, 0, 2 * CH:3 * CH].rearrange("p (s n) -> p s n", s=2)
        rest = e_ring[:, 2:4, :].rearrange("p a (s c) -> p (a s) c", s=2)
        xt = e_ring[:, 0, :].rearrange("p (s n c) -> p s n c", s=2, n=2)
        xxt = e_ring[:, 1, :].rearrange("p (s n c) -> p s n c", s=2, n=2)
        cx = e_ring[:, 2, :].rearrange("p (s n c) -> p s n c", s=2, n=2)
        rows = work[:, :].rearrange("p (t c) -> p t c", t=TILES)
        SEC = PAIRS * SLOTS
        hot_lo = e_ring[:, 0:2, :].rearrange("p a b -> p (a b)").bitcast(bf16).rearrange("p (j n) -> p j n", j=PAIRS)
        hot_hi = e_ring[:, 2:4, :].rearrange("p a b -> p (a b)").bitcast(bf16)[:, 0:3 * SEC].rearrange(
            "p (s j k) -> p s j k", s=3, j=PAIRS)
        XR = 8
        x_rows = view(e_ring, 5 * UW, [[C + E, XR], [1, C + E]])
        x_turned = view(e_ring, 4 * UW, [[C, 2], [1, C]])
        gelu1 = view(e_ring, 4 * UW + 2 * C, [[C, 2], [1, C]])
        gated = view(scratch, 4096, [[C, 2], [1, C]])
        gated_t = view(scratch, 4096 + 2 * C, [[C, 2], [1, C]])
        y_rows = view(scratch, 4096 + 4 * C, [[C, 4], [1, C]])
        y_back = work[:, :].rearrange("p (t c) -> p t c", t=TILES)
        COL = 11 * TILES * E
        POS, HI, LO = (COL + 128 + i * PAIRS for i in range(3))
        START = COL + 128 + 3 * PAIRS
        TILE_N = START + 4 * E
        OWN = TILE_N + E
        EXPERT = OWN + SLOTS * E
        EMPTY = EXPERT + SLOTS
        GATE = EMPTY + SLOTS
        OWN_GATE = GATE + SLOTS
        RANK = 32
        HUGE = 3.0e38
        v_all = work[:, :].rearrange("p (t c) -> p t c", t=TILES)

        GN_BANK = (5, 5, 7, 7)
        CONV_BANK = ((6, 7), (1, 4))

        def bank(i):
            return ps[:, i, :]

        def s_view(off, *dims):
            return view(scratch, off, dims)

        x_in = [sem(f"x_in{c}") for c in range(NCH)]
        first_in, conv_in, consts_in, w_in = sem("first_in"), sem("conv_in"), sem("consts_in"), sem("w_in")
        pool_init = sem("pool_init")
        gn_sums = [sem(f"gn_sums{k}") for k in range(4)]
        gn_group, gn_var, gn_rstd, gn_coef = (sem("gn_" + n) for n in ("group", "var", "rstd", "coef"))
        xhat_act, xhat_dve = sem("xhat_act"), sem("xhat_dve")
        dve_chain, act_chain = sem("dve_chain"), sem("act_chain")
        sq_done, n2_done, n2_floor, rn_done, fn_done = (sem(n) for n in ("sq_done", "n2_done", "n2_floor", "rn_done", "fn_done"))
        gram_done, gram_row = sem("gram_done"), sem("gram_row")
        gram_out = [sem(f"gram_out{c}") for c in range(NCH)]
        band_in = [sem(f"band_in{c}") for c in range(NCH)]
        parts_out = [sem(f"parts_out{n}") for n in range(4 * H)]
        cor_done, cor_tr, cor_t_done, y_done, relu_done, x1_done = (
            sem(n) for n in ("cor_done", "cor_tr", "cor_t_done", "y_done", "relu_done", "x1_done"))
        qk_done, part1, rest_done, part2, part3 = (
            sem(n) for n in ("qk_done", "part1", "rest_done", "part2", "part3"))
        v_done, v_stored = sem("v_done"), sem("v_stored")
        stack_in = [sem(f"stack_in{i}") for i in range(HPG)]
        scores_half, copy_done, max4_done, max2_done = (sem(n) for n in ("scores_half", "copy_done", "max4_done", "max2_done"))
        scores_done, max_done, sub_done, exp_done, sum4_done, sum2_done, sum_done, ln_done = (
            sem(n) for n in ("scores_done", "max_done", "sub_done", "exp_done", "sum4_done",
                             "sum2_done", "sum_done", "ln_done"))
        r_done, norm_pool, norm_dve, pv_done = (sem(n) for n in ("r_done", "norm_pool", "norm_dve", "pv_done"))
        v_slot_ready = [sem(f"v_slot_ready{i}") for i in range(HPG)]
        acc_out, acc_tr, x2_added = (sem(n) for n in ("acc_out", "acc_tr", "x2_added"))
        tr2_done, xt_done, cx_done, cx_out, xx_done, xx_out, o_done, x3_done, xsum_done = (
            sem(n) for n in ("tr2_done", "xt_done", "cx_done", "cx_out", "xx_done", "xx_out", "o_done", "x3_done",
                             "xsum_done"))
        logits_done, logits_read, shifted, gate_exp, comb_done, gate_own, gate_done = (
            sem(n) for n in ("logits_done", "logits_read", "shifted", "gate_exp", "comb_done", "gate_own", "gate_done"))
        h_done, gelu_done, gated_done, gtr_done, gt_done, ye_done, ye_out = (
            sem(n) for n in ("h_done", "gelu_done", "gated_done", "gtr_done", "gt_done", "ye_done", "ye_out"))
        rtr_done, row_done, row_out, zero_out = sem("rtr_done"), sem("row_done"), sem("row_out"), sem("zero_out")
        mask_done, ranks_done, places_done, tiles_hot, tiles_scaled, hots_done, slots_done, plan_done = (
            sem(n) for n in ("mask_done", "ranks_done", "places_done", "tiles_hot", "tiles_scaled", "hots_done",
                             "slots_done", "plan_done"))
        experts_done = sem("experts_done")
        xr_in = [sem(f"xr_in{i}") for i in range(XR)]
        y_out = sem("y_out")
        xtr_done, xt_out = sem("xtr_done"), sem("xt_out")
        y_in = [sem(f"y_in{b}") for b in range(B)]
        ytr_done, x4_done, out_done = sem("ytr_done"), sem("x4_done"), sem("out_done")

        def slot_steps(eng, step):
            inside = lambda k: not isinstance(k, int) or 0 <= k < SLOTS
            for s in range(7):
                step(s, s, inside)
            with eng.Fori(0, (SLOTS - 7) // XR) as i:
                for r in range(7, 7 + XR):
                    step(i * XR + r, r % XR, inside)
            for s in range(SLOTS, SLOTS + 3):
                step(s, s % XR, inside)

        def attention_steps(eng, step):
            for u in range(UPG):
                step(u, u, 0, lambda k: k <= u)
            with eng.Fori(1, NG) as g:
                for u in range(UPG):
                    step(g * UPG + u, u, g, lambda k: True)
            for u in range(LAG):
                step(UNITS + u, u, NG, lambda k: k > u)

        def pooled(U):
            return POOLED_LAST if isinstance(U, int) and U >= UNITS - 4 else POOLED

        def later_than(U, k):
            return not isinstance(U, int) or U >= k

        assert (SLOTS - 7) % XR == 0
        block = ctx.enter_context(nc.Block())
        FIRST, CONV, LATER = 3, 4, 9

        @block.sync
        def _(sp):
            for c in range(NCH):
                for h in range(H):
                    sp.dma_start(x_res[:, h, c * CH:(c + 1) * CH].rearrange("p (b n) -> p b n", b=BPC),
                                 x[c * BPC:(c + 1) * BPC, h * P:(h + 1) * P].rearrange("b p y x -> p b (y x)")
                                 ).then_inc(x_in[c], 16)
                if c == 0:
                    for dst, src in ((conv_wT_sb[:], conv_wT.rearrange("h p o -> p h o")), (mask_sb[:], edge_mask),
                                     (conv_cT_sb[:], conv_cT), (conv_b_sb[:], conv_b)):
                        sp.dma_start(dst, src).then_inc(conv_in, 16)
            later = ((qkv_sb[:], qkv_blocks.rearrange("s p o -> p s o")), (qk_bias_sb[:], qk_bias), (v_bias_sb[:], v_bias),
                     (gram_wT_sb[:], gram_wT.rearrange("h p o -> p h o")), (gamma_sb[:], gamma),
                     (gate_sb[:], gate_wT.rearrange("(h p) e -> p h e", p=P)), (rank_sb[:], expert_rank),
                     (before_sb[:], before), (tab[:], tables))
            for dst, src in later:
                sp.dma_start(dst, src).then_inc(consts_in, 16)
            sp.wait_ge(pool_init, 2)
            zeros = v_slot[:, :].rearrange("p a h d -> p (a h d)")
            sp.dma_start(row_dram[T:YROWS], zeros[:, 0:C + E]).then_inc(zero_out, 16)
            sp.dma_start(y_dram[T:YROWS], zeros[:, 0:C]).then_inc(zero_out, 16)
            for i in range(2):
                sp.dma_start(y_dram[i * T // 2:(i + 1) * T // 2].rearrange("(p r) c -> p (r c)", p=P), zeros).then_inc(zero_out, 16)
            for c in range(NCH):
                sp.wait_ge(gram_row, TPC * (c + 1))
                sp.dma_start(gram_dram[c * TPC:(c + 1) * TPC].rearrange("t p r -> p t r"),
                             view(scratch, GST + (c % 2) * TPC * ROW, [[ROW, TPC], [1, ROW]])
                             ).then_inc(gram_out[c], 16)
                sp.wait_ge(gram_out[c], 16)
                skew = bass.AP(gram_dram.tensor, c * TPC * P * ROW, [[ROW + 1, P], [P * ROW, TPC], [1, WIN]])
                sp.dma_start(view(scratch, BAND + c * TPC * WIN, [[WIN, TPC], [1, WIN]]), skew
                             ).then_inc(band_in[c], 16)

            def load_stack(g, i):
                row = (g * HPG + i) * D * T
                for a in range(PARTS):
                    rows_a = slice(a * PARTS * D, (a + 1) * PARTS * D)
                    q_src = bass.AP(part_dram.tensor, row, [[C * T, PARTS], [T, D], [1, T]])
                    k_src = bass.AP(part_dram.tensor, row + (PARTS + a) * C * T, [[0, PARTS], [T, D], [1, T]])
                    sp.dma_start(q_stack[rows_a, i, :], q_src).then_inc(stack_in[i], 16)
                    sp.dma_start(k_stack[rows_a, i, :], k_src).then_inc(stack_in[i], 16)

            for n in range(4 * H):
                sp.wait_ge(part3, NCH // 2 * (n + 1))
                h, s, cols = n // 4, n // 2 % 2, slice(n % 2 * (T // 2), (n % 2 + 1) * (T // 2))
                dst = bass.AP(part_dram.tensor, (s * PARTS * C + h * P) * T + n % 2 * (T // 2), [[T, P], [C * T, PARTS], [1, T // 2]])
                sp.dma_start(dst, parts[:, s, :, cols]).then_inc(parts_out[n], 16)
                if n == 3:
                    for i in range(4):
                        sp.wait_ge(parts_out[i], 16)
                    for i in range(HPG):
                        load_stack(0, i)
            for n in range(4, 8):
                sp.wait_ge(parts_out[n], 16)
            weights = ((w13_sb[:, 0, :], w13T[0]), (w13_sb[:, 1, :], w13T[1]), (w2_sb[:, 0, :], w2T[0]), (w2_sb[:, 1, :], w2T[1]))
            for i in range(HPG):
                sp.wait_ge(scores_done, 4 * (i + 1))
                load_stack(1, i)
                sp.dma_start(*weights[i]).then_inc(w_in, 16)
            with sp.Fori(1, NG - 1) as g:
                for i in range(HPG):
                    sp.wait_ge(scores_done, g * UPG + 4 * (i + 1))
                    load_stack(g + 1, i)
            for c in range(NCH):
                sp.wait_ge(row_done, BPC * (c + 1))
                sp.dma_start(row_dram[c * CH:(c + 1) * CH, 0:C].rearrange("(t p) c -> p t c", p=P),
                             rows[:, c * TPC:(c + 1) * TPC]).then_inc(row_out, 16)
            sp.wait_ge(comb_done, 1)
            sp.dma_start(row_dram[0:T, C:C + E].rearrange("(t p) e -> p t e", p=P),
                         s_view(7 * TILES * E, [E, TILES], [1, E])).then_inc(row_out, 16)
            sp.wait_ge(y_out, 16 * SLOTS)
            for b in range(B):
                sp.dma_start(y_back[:, H * b:H * (b + 1)], y_dram[b * N:(b + 1) * N].rearrange("(t p) c -> p t c", p=P)
                             ).then_inc(y_in[b], 16)
            for b in range(B):
                sp.wait_ge(x4_done, b + 1)
                sp.dma_start(out[b].rearrange("(h p) y x -> p h (y x)", p=P),
                             x_res[:, :, b * N:(b + 1) * N]).then_inc(out_done, 16)
            sp.wait_ge(out_done, 16 * B)

        @block.gpsimd
        def _(pool):
            nc.gpsimd.memset(view(scratch, GST, [[1, 2 * TPC * ROW]]), 0.0).then_inc(pool_init, 1)
            nc.gpsimd.memset(v_slot[:], 0.0).then_inc(pool_init, 1)
            pool.wait_ge(pool_init, 2)
            for n in range(2 * H * NCH):
                s, c = n // NCH, n % NCH
                pool.wait_ge(part2, n + 1)
                nc.gpsimd.tensor_tensor(parts[:, s % 2, 2, c * CH:(c + 1) * CH], rest[:, n % 4],
                                        parts[:, s % 2, 1, c * CH:(c + 1) * CH], ALU.subtract).then_inc(part3, 1)
            def weights(U, u):
                pool.wait_ge(r_done, U + 1)
                n = pooled(U)
                ev = e_ring[:, u % ER, :].rearrange("p (b n) -> p b n", b=B)[:, :, 0:n]
                nc.gpsimd.tensor_tensor(ev, ev, view(s_inv, (u % 2) * P, [[0, B], [1, n]]), ALU.mult).then_inc(norm_pool, 1)

            with pool.Fori(0, NG - 1) as g:
                for u in range(UPG):
                    weights(g * UPG + u, u)
            for u in range(UPG):
                weights((NG - 1) * UPG + u, u)
            for b in range(B):
                pool.wait_ge(xhat_act, B * 2 + b + 1)
                pool.wait_ge(xhat_dve, B * 2 + b + 1)
                nc.gpsimd.tensor_tensor(x_res[:, :, b * N:(b + 1) * N], x_res[:, :, b * N:(b + 1) * N],
                                        x_hat[:, :, b * N:(b + 1) * N], ALU.add).then_inc(xsum_done, 1)
            pool.wait_ge(tiles_hot, 1)
            nc.gpsimd.tensor_tensor(hot_hi[:, 0], hot_hi[:, 2], view(tab, TILE0, [[1, PAIRS], [0, SLOTS]]),
                                    ALU.mult).then_inc(tiles_scaled, 1)
            pool.wait_ge(plan_done, 1)
            pool.wait_ge(row_out, 16 * (NCH + 1))
            pool.wait_ge(zero_out, 16 * 4)

            def gather(k):
                if k >= XR:
                    pool.wait_ge(xtr_done, k - XR + 1)
                    pool.wait_ge(gate_done, k - XR + 1)
                nc.gpsimd.indirect_dma_start(out=x_rows[:, k % XR], out_offset=None, in_=row_dram[:, :],
                                             in_offset=bass.IndirectOffsetOnAxis(ap=slot_x[:, k:k + 1], axis=0)
                                             ).then_inc(xr_in[k % XR], 16)

            for k in range(XR):
                gather(k)
            for k in range(SLOTS):
                pool.wait_ge(ye_out, k + 1)
                if k >= 1:
                    pool.wait_ge(y_out, 16 * k)
                nc.gpsimd.indirect_dma_start(out=y_dram[:, :], in_=y_rows[:, k % 4], in_offset=None,
                                             out_offset=bass.IndirectOffsetOnAxis(ap=slot_x[:, k:k + 1], axis=0),
                                             compute_op=ALU.add).then_inc(y_out, 16)
                if k + XR < SLOTS:
                    gather(k + XR)

        @block.scalar
        def _(act):
            chain = [0]

            def link(ins):
                chain[0] += 1
                ins.then_inc(act_chain, 1)
                act.wait_ge(act_chain, chain[0])

            for dst, src in ((group_sb[:], group_ones), (ones_sb[:], ones), (ident[:], identity)):
                act.dma_start(dst, src).then_inc(first_in, 16)

            def power(dst, src, done):
                link(nc.scalar.activation(dst, src, ACT.Ln))
                nc.scalar.activation(dst, dst, ACT.Exp, scale=-0.5).then_inc(done, 1)

            def deviation(k, c):
                act.wait_ge(gn_var, NCH * k + c + 1)
                power(gn[:, c, 2], gn[:, c, 1], gn_rstd)

            def normalise(k, c):
                act.wait_ge(gn_coef, NCH * k + c + 1)
                for i in range(BPC):
                    cols = slice((c * BPC + i) * N, (c * BPC + i + 1) * N)
                    nc.scalar.activation(x_hat[:, 0, cols], x_res[:, 0, cols], ACT.Identity,
                                         bias=gn[:, c, 3, i:i + 1], scale=gn[:, c, 2, i:i + 1]).then_inc(xhat_act, 1)

            nc.scalar.preload_act_table_set("natural_log_exp_and_others")
            act.wait_ge(first_in, 16 * FIRST)
            nc.scalar.activation(ident_neg[:], ident[:], ACT.Copy, scale=-1.0)

            def squares_of(c):
                act.wait_ge(xhat_act, BPC * (c + 1))
                act.wait_ge(xhat_dve, BPC * (c + 1))
                nc.scalar.activation(view(work, c * CH, [[T, H], [1, CH]]), x_hat[:, :, c * CH:(c + 1) * CH],
                                     ACT.Square).then_inc(sq_done, 1)

            def gram_rows(c):
                for t in range(TPC):
                    i, hb = c * TPC + t, t % 2
                    act.wait_ge(gram_done, i + 1)
                    if i == 0:
                        act.wait_ge(pool_init, 1)
                    if t == 0 and c >= 2:
                        act.wait_ge(gram_out[c - 2], 16)
                    off = GST + (c % 2) * TPC * ROW + t * ROW + (0 if hb else REACH)
                    nc.scalar.activation(view(scratch, off, [[1, ROW - REACH]]), ps[:, 2 + i % 2, 0:ROW - REACH],
                                         ACT.Copy).then_inc(gram_row, 1)

            def turned_correlations(d):
                act.wait_ge(cor_tr, d + 1)
                nc.scalar.activation(cor_t[:, d * CH:(d + 1) * CH], ps[0:NK, 0, :], ACT.Copy).then_inc(cor_t_done, 1)

            def conv_out(d):
                if d == 0:
                    act.wait_ge(conv_in, 16 * CONV)
                for o in range(H):
                    act.wait_ge(y_done, H * d + o + 1)
                    if d >= 1:
                        act.wait_ge(x1_done, d)
                    nc.scalar.activation(view(scratch, YB + o * CH, [[1, CH]]), bank(CONV_BANK[d % 2][o]), ACT.Relu,
                                         bias=conv_b_sb[:, o:o + 1]).then_inc(relu_done, 1)

            deviation(0, 0)
            normalise(0, 0)
            squares_of(0)
            for t in range(NCH + 1):
                if t < NCH:
                    act.wait_ge(n2_floor, t + 1)
                    power(rnorm, rnorm, rn_done)
                if t < NCH:
                    gram_rows(t)
                if t + 1 < NCH:
                    deviation(0, t + 1)
                    normalise(0, t + 1)
                    squares_of(t + 1)
                if 0 <= t - 1 < NCH:
                    turned_correlations(t - 1)
                if 0 <= t - 2:
                    deviation(1, t - 2)
                    normalise(1, t - 2)
                if 0 <= t - 1 < NCH:
                    conv_out(t - 1)
            act.wait_ge(consts_in, 16 * LATER)
            nc.scalar.activation(before_bf[:], before_sb[:], ACT.Copy).then_inc(act_chain, 1)
            nc.scalar.activation(ones_bf[:], ones_sb[:], ACT.Copy).then_inc(act_chain, 1)
            chain[0] += 2
            def second_part(n):
                s, c = n // NCH, n % NCH
                act.wait_ge(rest_done, n + 1)
                nc.scalar.activation(parts[:, s % 2, 1, c * CH:(c + 1) * CH], rest[:, n % 4], ACT.Copy).then_inc(part2, 1)

            for n in range(2 * H * NCH):
                s, c = n // NCH, n % NCH
                if c % 2 == 0 and s >= 2:
                    act.wait_ge(parts_out[2 * (s - 2) + c // 2], 16)
                act.wait_ge(qk_done, n + 1)
                nc.scalar.activation(parts[:, s % 2, 0, c * CH:(c + 1) * CH], bank(n % 4), ACT.Identity,
                                     bias=qk_bias_sb[:, s % 2:s % 2 + 1]).then_inc(part1, 1)
                if n == 0:
                    deviation(1, NCH - 1)
                    normalise(1, NCH - 1)
                if n >= 1:
                    second_part(n - 1)
            second_part(2 * H * NCH - 1)

            def fill_v(g, i):
                nc.scalar.activation(view(v_slot, i * (HPG * D + D), [[HPG * HPG * D, B * H], [1, D]]),
                                     view(work, g * (HPG * D) + i * D, [[C, B * H], [1, D]]),
                                     ACT.Copy).then_inc(v_slot_ready[i], 1)

            def copy_scores(U, u):
                act.wait_ge(scores_half, U + 1)
                if later_than(U, 2):
                    act.wait_ge(max4_done, U - 1)
                nc.scalar.activation(score_bf[:, u % 2], bank(2 * (u % 2) + 1), ACT.Copy).then_inc(copy_done, 1)

            def exponentials(U, u):
                act.wait_ge(sub_done, U + 1)
                if later_than(U, ER):
                    act.wait_ge(pv_done, U - ER + 1)
                nc.scalar.activation(e_ring[:, u % ER, :], ps[:, 2 * (u % 2):2 * (u % 2) + 2, :], ACT.Exp
                                     ).then_inc(exp_done, 1)

            def logarithm(U, u):
                act.wait_ge(sum_done, U + 1)
                nc.scalar.activation(s_ln[:, u % 2], ps[:, 6 + u % 2, 0:P], ACT.Ln).then_inc(ln_done, 1)

            def inverse(U, u):
                act.wait_ge(ln_done, U + 1)
                if later_than(U, 2):
                    act.wait_ge(norm_pool, U - 1)
                    act.wait_ge(norm_dve, U - 1)
                nc.scalar.activation(s_inv[:, u % 2], s_ln[:, u % 2], ACT.Exp, scale=-1.0).then_inc(r_done, 1)

            def evacuate(g):
                act.wait_ge(pv_done, g * UPG)
                nc.scalar.activation(o_sb, bank(4), ACT.Copy).then_inc(acc_out, 1)

            def attention_step(U, u, g, has):
                if has(4):
                    logarithm(U - 4, (u - 4) % UPG)
                if has(0):
                    copy_scores(U, u)
                if has(4):
                    inverse(U - 4, (u - 4) % UPG)
                if has(1):
                    exponentials(U - 1, (u - 1) % UPG)
                if u == LAG - 1 and has(LAG):
                    evacuate(g)
                if u in (0, 1, 2, LAG) and has(u + 1) and has(0):
                    i = min(u, HPG - 1)
                    act.wait_ge(pv_done, g * UPG - 4 * (HPG - 1 - i))
                    fill_v(g, i)

            act.wait_ge(v_stored, TILES)
            act.wait_ge(pool_init, 2)
            act.wait_ge(part3, 2 * H * NCH)
            for i in range(HPG):
                fill_v(0, i)
            attention_steps(act, attention_step)
            deviation(2, 0)
            normalise(2, 0)

            def row_copy(j):
                act.wait_ge(rtr_done, j + 1)
                nc.scalar.activation(rows[:, 2 * j:2 * j + 2], ps[:, 5, :].rearrange("p (t c) -> p t c", t=2),
                                     ACT.Copy).then_inc(row_done, 1)

            for b in range(B + 1):
                if b < B:
                    act.wait_ge(tr2_done, b + 1)
                    nc.scalar.activation(xt[:, b % 2], bank(b % 2), ACT.Copy).then_inc(xt_done, 1)
                    act.wait_ge(xx_done, b + 1)
                    if b >= 2:
                        act.wait_ge(o_done, b - 1)
                    nc.scalar.activation(xxt[:, b % 2], bank(2), ACT.Copy).then_inc(xx_out, 1)
                if b + 1 < NCH:
                    deviation(2, b + 1)
                    normalise(2, b + 1)
                if b >= 4:
                    row_copy(b - 4)
                if b >= 3 and b % 2 == 1:
                    deviation(3, (b - 3) // 2)
                    normalise(3, (b - 3) // 2)
            deviation(3, NCH - 1)
            normalise(3, NCH - 1)
            row_copy(B - 3)
            act.wait_ge(shifted, 1)
            nc.scalar.activation(s_view(COL + 4 * TILES, [1, TILES]), s_view(COL + 3 * TILES, [1, TILES]), ACT.Exp
                                 ).then_inc(gate_exp, 1)
            row_copy(B - 2)
            row_copy(B - 1)

            nc.scalar.preload_act_table(ACT.Gelu)

            def slot_step(s, r, body):
                if body(s):
                    act.wait_ge(xtr_done, s + 1)
                    if not isinstance(s, int) or s >= 2:
                        act.wait_ge(h_done, s - 1)
                    nc.scalar.activation(x_turned[:, r % 2], ps[:, 2 + r % 2, 0:C], ACT.Copy).then_inc(xt_out, 1)
                if body(s - 1):
                    act.wait_ge(h_done, s)
                    if not isinstance(s, int) or s >= 3:
                        act.wait_ge(gated_done, s - 2)
                    nc.scalar.activation(gelu1[:, (r + 1) % 2], ps[:, (r + 1) % 2, 0:C], ACT.Gelu).then_inc(gelu_done, 1)
                if body(s - 2):
                    act.wait_ge(gtr_done, s - 1)
                    if not isinstance(s, int) or s >= 4:
                        act.wait_ge(ye_done, s - 3)
                    nc.scalar.activation(gated_t[:, r % 2], ps[:, 4 + r % 2, 0:C], ACT.Copy).then_inc(gt_done, 1)

            slot_steps(act, slot_step)

        @block.vector
        def _(dve):
            chain = [0]

            def count(ins):
                chain[0] += 1
                ins.then_inc(dve_chain, 1)

            def link(*all_ins):
                for ins in all_ins:
                    count(ins)
                dve.wait_ge(dve_chain, chain[0])

            def statistics(k, c):
                for h in range(H):
                    for i in range(BPC):
                        b = c * BPC + i
                        count(nc.vector.bn_stats(stats[:, c, h * BPC + i], x_res[:, h, b * N:(b + 1) * N]))
                dve.wait_ge(dve_chain, chain[0])
                square, mean, scaled = (view(stats, c * SPC * 6 + i, [[6, SPC], [3, 2]]) for i in range(3))
                link(nc.vector.tensor_tensor(square, mean, mean, ALU.mult))
                nc.vector.scalar_tensor_tensor(out=square, in0=scaled, scalar=2.0 / N, in1=square, op0=ALU.mult,
                                               op1=ALU.add).then_inc(gn_sums[k], 1)

            def variance(k, c):
                dve.wait_ge(gn_group, NCH * k + c + 1)
                pg = view(ps, GN_BANK[k] * CH, [[2, SPC], [1, 2]])
                mean, var = gn[:, c, 0], gn[:, c, 1]
                link(nc.vector.tensor_copy(mean, pg[:, :, 1]))
                link(nc.vector.tensor_tensor(gn_tmp[:], mean, mean, ALU.mult))
                link(nc.vector.tensor_tensor(var, pg[:, :, 0], gn_tmp[:], ALU.subtract))
                nc.vector.tensor_scalar(var, var, 0.0, EPS, ALU.max, ALU.add).then_inc(gn_var, 1)

            def second_half(k, c):
                dve.wait_ge(gn_rstd, NCH * k + c + 1)
                mean, var, rstd = (gn[:, c, i] for i in range(3))
                link(nc.vector.scalar_tensor_tensor(out=gn_tmp[:], in0=rstd, scalar=-0.5, in1=rstd, op0=ALU.mult, op1=ALU.mult))
                link(nc.vector.tensor_tensor(gn_tmp[:], gn_tmp[:], var, ALU.mult))
                link(nc.vector.scalar_tensor_tensor(out=rstd, in0=gn_tmp[:], scalar=1.5, in1=rstd, op0=ALU.add, op1=ALU.mult))
                nc.vector.scalar_tensor_tensor(out=gn[:, c, 3], in0=mean, scalar=-1.0, in1=rstd, op0=ALU.mult,
                                               op1=ALU.mult).then_inc(gn_coef, 1)
                dve.wait_ge(gn_coef, NCH * k + c + 1)
                for i in range(BPC):
                    cols = slice((c * BPC + i) * N, (c * BPC + i + 1) * N)
                    nc.vector.tensor_scalar(x_hat[:, 1, cols], x_res[:, 1, cols], gn[:, c, 2, BPC + i:BPC + i + 1],
                                            gn[:, c, 3, BPC + i:BPC + i + 1], ALU.mult, ALU.add).then_inc(xhat_dve, 1)

            def floor_of_norms(c):
                dve.wait_ge(n2_done, c + 1)
                nc.vector.tensor_scalar(rnorm, bank(0), EPS_NORM2, None, ALU.max).then_inc(n2_floor, 1)

            def unit_vectors(c):
                nc_cols = slice(c * CH, (c + 1) * CH)
                dve.wait_ge(rn_done, c + 1)
                nc.vector.tensor_tensor(view(work, c * CH, [[T, H], [1, CH]]), x_hat[:, :, nc_cols],
                                        view(scratch, 0, [[0, H], [1, CH]]), ALU.mult).then_inc(fn_done, 1)
                dve.wait_ge(fn_done, c + 1)

            def correlations(d):
                dve.wait_ge(band_in[d], 16)
                if d == 0:
                    dve.wait_ge(conv_in, 16 * CONV)
                nc.vector.tensor_tensor(view(scratch, COR + d * TPC * NK, [[NK, TPC], [K, K], [1, K]]),
                                        view(scratch, BAND + d * TPC * WIN, [[WIN, TPC], [1, K], [SIDE, K]]),
                                        view(mask_sb, 0, [[0, TPC], [1, K], [0, K]]), ALU.mult).then_inc(cor_done, 1)

            def add_conv(d):
                dve.wait_ge(relu_done, H * (d + 1))
                xr = x_res[:, :, d * CH:(d + 1) * CH]
                nc.vector.tensor_tensor(xr, xr, view(scratch, YB, [[CH, H], [1, CH]]), ALU.add).then_inc(x1_done, 1)
                dve.wait_ge(x1_done, d + 1)

            dve.wait_ge(x_in[0], 16 * H)
            statistics(0, 0)
            variance(0, 0)
            second_half(0, 0)
            dve.wait_ge(x_in[1], 16 * H)
            statistics(0, 1)
            for t in range(NCH + 2):
                if t < NCH:
                    floor_of_norms(t)
                if t == NCH:
                    correlations(t - 1)
                if 0 <= t - 2:
                    add_conv(t - 2)
                if t < NCH:
                    unit_vectors(t)
                if 0 <= t - 2:
                    statistics(1, t - 2)
                if t + 1 < NCH:
                    variance(0, t + 1)
                if 0 <= t - 1 < NCH - 1:
                    correlations(t - 1)
                if t + 2 < NCH:
                    dve.wait_ge(x_in[t + 2], 16 * H)
                    statistics(0, t + 2)
                if t + 1 < NCH:
                    second_half(0, t + 1)
                if 0 <= t - 2:
                    variance(1, t - 2)
                    second_half(1, t - 2)
            dve.wait_ge(consts_in, 16 * LATER)
            for n in range(2 * H * NCH):
                s, c = n // NCH, n % NCH
                dve.wait_ge(part1, n + 1)
                if n >= 4:
                    dve.wait_ge(part3, n - 3)
                nc.vector.scalar_tensor_tensor(out=rest[:, n % 4], in0=bank(n % 4), scalar=qk_bias_sb[:, s % 2:s % 2 + 1],
                                               in1=parts[:, s % 2, 0, c * CH:(c + 1) * CH], op0=ALU.add,
                                               op1=ALU.subtract).then_inc(rest_done, 1)
                dve.wait_ge(v_done, n + 1)
                nc.vector.tensor_tensor(v_all[:, n].rearrange("p (r d) -> p r d", d=D),
                                        ps[:, 6 + n % 2, 0:C].rearrange("p (r d) -> p r d", d=D),
                                        view(v_bias_sb, 0, [[0, HEADS], [1, D]]), ALU.add).then_inc(v_stored, 1)

            def half(ap, k, width):
                return ap[:, k * width:(k + 1) * width]

            def maximum4(U, u):
                dve.wait_ge(copy_done, U + 1)
                dve.wait_ge(scores_done, U + 1)
                if later_than(U, 1):
                    dve.wait_ge(max2_done, U)
                nc.vector.tensor_tensor(max4, bank(2 * (u % 2)), score_bf[:, u % 2], ALU.max).then_inc(max4_done, 1)

            def maximum2(U, u):
                dve.wait_ge(max4_done, U + 1)
                if later_than(U, 1):
                    dve.wait_ge(max_done, U)
                nc.vector.tensor_tensor(max2, half(max4, 0, 2 * P), half(max4, 1, 2 * P), ALU.max).then_inc(max2_done, 1)

            def maximum1(U, u):
                dve.wait_ge(max2_done, U + 1)
                if later_than(U, 2):
                    dve.wait_ge(sub_done, U - 1)
                nc.vector.tensor_tensor(m_bf[:, u % 2], half(max2, 0, P), half(max2, 1, P), ALU.max).then_inc(max_done, 1)

            def total4(U, u):
                dve.wait_ge(exp_done, U + 1)
                if later_than(U, 2):
                    dve.wait_ge(sum2_done, U - 1)
                e = e_ring[:, u % ER, :]
                nc.vector.tensor_tensor(sum4[:, u % 2], half(e, 0, 4 * P), half(e, 1, 4 * P), ALU.add).then_inc(sum4_done, 1)

            def total2(U, u):
                dve.wait_ge(sum4_done, U + 1)
                if later_than(U, 2):
                    dve.wait_ge(sum_done, U - 1)
                nc.vector.tensor_tensor(sum2[:, u % 2], half(sum4[:, u % 2], 0, 2 * P), half(sum4[:, u % 2], 1, 2 * P), ALU.add
                                        ).then_inc(sum2_done, 1)

            def weights(U, u):
                dve.wait_ge(r_done, U + 1)
                n = pooled(U)
                e = e_ring[:, u % ER, :].rearrange("p (b n) -> p b n", b=B)[:, :, n:]
                nc.vector.tensor_tensor(e, e, view(s_inv, (u % 2) * P + n, [[0, B], [1, P - n]]),
                                        ALU.mult).then_inc(norm_dve, 1)

            def add_heads(g, group):
                dve.wait_ge(acc_tr, group)
                xr = view(x_res, g * (HPG * D) - HPG * D, [[T, H], [N, B], [1, HPG * D]])
                nc.vector.tensor_tensor(xr, xr, view(ps, 5 * CH, [[N, H], [HPG * D, B], [1, HPG * D]]),
                                        ALU.add).then_inc(x2_added, 1)

            def attention_step(U, u, g, has):
                if has(0):
                    maximum4(U, u)
                if has(5):
                    weights(U - 5, (u - 5) % UPG)
                if has(0):
                    maximum2(U, u)
                    maximum1(U, u)
                if has(1):
                    total4(U - 1, (u - 1) % UPG)
                if has(2):
                    total2(U - 2, (u - 2) % UPG)
                if u == LAG + 2 and has(LAG + 3):
                    add_heads(g, g)

            attention_steps(dve, attention_step)
            add_heads(NG, NG)

            dve.wait_ge(x2_added, NG)
            statistics(2, 0)
            statistics(2, 1)
            variance(2, 0)
            second_half(2, 0)
            def choose(c, chunks, call):
                tiles = chunks * TPC

                def per_token(i):
                    return s_view(i * TILES * E + c * TPC * E, [E, tiles], [1, E])

                def column(i):
                    return s_view(COL + i * TILES + c * TPC, [1, tiles], [0, E])

                def best(logit, top, hot):
                    col, first = (s_view(COL + i * TILES + c * TPC, [1, tiles]) for i in (top, 2))
                    link(nc.vector.tensor_reduce(col, per_token(logit), AX, ALU.max))
                    link(nc.vector.tensor_tensor(per_token(3), per_token(logit), column(top), ALU.is_equal))
                    link(nc.vector.tensor_tensor(per_token(3), per_token(3), view(rank_sb, 0, [[0, tiles], [1, E]]), ALU.mult))
                    link(nc.vector.tensor_reduce(first, per_token(3), AX, ALU.max))
                    link(nc.vector.tensor_tensor(per_token(hot), per_token(3), column(2), ALU.is_equal))

                dve.wait_ge(logits_done, c + chunks)
                nc.vector.tensor_copy(per_token(0), ps[:, 6, c * TPC * E:(c * TPC + tiles) * E].rearrange("p (t e) -> p t e", e=E)
                                      ).then_inc(logits_read, 1)
                dve.wait_ge(logits_read, call)
                best(0, 0, 4)
                link(nc.vector.scalar_tensor_tensor(out=per_token(1), in0=per_token(4), scalar=-HUGE, in1=per_token(0),
                                                    op0=ALU.mult, op1=ALU.add))
                best(1, 1, 5)
                nc.vector.tensor_tensor(mask_bf[:, c * TPC:c * TPC + tiles], per_token(4), per_token(5), ALU.add
                                        ).then_inc(mask_done, 1)

            for b in range(B + 1):
                if b < B:
                    dve.wait_ge(cx_done, b + 1)
                    if b >= 2:
                        dve.wait_ge(o_done, b - 1)
                    nc.vector.tensor_copy(cx[:, b % 2], ps[:, 3, :].rearrange("p (n c) -> p n c", n=2)).then_inc(cx_out, 1)
                if b >= 1:
                    dve.wait_ge(o_done, b)
                    dve.wait_ge(xsum_done, b)
                    xr = x_res[:, :, (b - 1) * N:b * N]
                    nc.vector.scalar_tensor_tensor(out=xr, in0=ps[:, 4, :].rearrange("p (h n) -> p h n", h=H),
                                                   scalar=gamma_sb[:, 0:1], in1=xr, op0=ALU.mult, op1=ALU.add
                                                   ).then_inc(x3_done, 1)
                if b == 2:
                    dve.wait_ge(x3_done, b)
                    statistics(3, 0)
                if b + 1 < NCH:
                    if b == 1:
                        statistics(2, b + 2)
                    variance(2, b + 1)
                    second_half(2, b + 1)
                    if b == 0:
                        statistics(2, b + 2)
                if b >= 4 and b % 2 == 0:
                    dve.wait_ge(x3_done, b)
                    statistics(3, (b - 2) // 2)
                if b == 3 or b == 5 or b == 7:
                    variance(3, (b - 3) // 2)
                    second_half(3, (b - 3) // 2)
                if b == 6:
                    choose(0, 1, 1)
            variance(3, 3)
            second_half(3, 3)
            choose(1, 2, 2)
            choose(3, 1, 3)

            def col(i):
                return s_view(COL + i * TILES, [1, TILES])

            def per_token(i):
                return s_view(i * TILES * E, [E, TILES], [1, E])

            def column(i):
                return s_view(COL + i * TILES, [1, TILES], [0, E])

            def starts(buf, back, *dims):
                return s_view(START + buf * 2 * E + E - back, *(dims or ([1, E],)))

            nc.vector.tensor_tensor(col(3), col(1), col(0), ALU.subtract).then_inc(shifted, 1)
            count(nc.vector.memset(starts(0, E, [1, 4 * E]), 0.0))
            dve.wait_ge(ranks_done, NCH)
            link(nc.vector.tensor_scalar(s_view(TILE_N, [1, E]), ps[:, 7, RANK + TILES * E:RANK + (TILES + 1) * E],
                                         1.0 / P, (P - 1) / (2.0 * P), ALU.mult, ALU.add))
            dve.wait_ge(gate_exp, 1)
            link(nc.vector.tensor_scalar(s_view(TILE_N, [1, E]), s_view(TILE_N, [1, E]), ROUND, None, ALU.add),
                 nc.vector.tensor_scalar(col(5), col(4), 1.0, None, ALU.add))
            link(nc.vector.tensor_scalar(starts(0, 0), s_view(TILE_N, [1, E]), ROUND, None, ALU.subtract),
                 nc.vector.reciprocal(col(6), col(5)))
            link(nc.vector.tensor_tensor(starts(1, 0), starts(0, 0), starts(0, 1), ALU.add),
                 nc.vector.tensor_tensor(col(7), col(4), col(6), ALU.mult))
            link(nc.vector.tensor_tensor(starts(0, 0), starts(1, 0), starts(1, 2), ALU.add),
                 nc.vector.tensor_tensor(per_token(6), per_token(4), column(6), ALU.mult))
            link(nc.vector.tensor_tensor(starts(1, 0), starts(0, 0), starts(0, 4), ALU.add),
                 nc.vector.tensor_tensor(per_token(7), per_token(5), column(7), ALU.mult))
            link(nc.vector.scalar_tensor_tensor(out=per_token(8), in0=starts(1, 1, [0, TILES], [1, E]), scalar=float(P),
                                                in1=ps[:, 7, RANK:RANK + TILES * E].rearrange("p (t e) -> p t e", e=E),
                                                op0=ALU.mult, op1=ALU.add))
            nc.vector.tensor_tensor(per_token(7), per_token(6), per_token(7), ALU.add).then_inc(comb_done, 1)
            link(nc.vector.tensor_tensor(s_view(9 * TILES * E, [TILES * E, TOP], [1, TILES * E]),
                                         s_view(4 * TILES * E, [TILES * E, TOP], [1, TILES * E]),
                                         s_view(8 * TILES * E, [0, TOP], [1, TILES * E]), ALU.mult))
            pos, hi, lo = (s_view(o, [1, PAIRS]) for o in (POS, HI, LO))
            link(nc.vector.tensor_reduce(pos, s_view(9 * TILES * E, [E, PAIRS], [1, E]), AX, ALU.add))
            link(nc.vector.tensor_scalar(hi, pos, 1.0 / P, -(P - 1) / (2.0 * P), ALU.mult, ALU.add))
            link(nc.vector.tensor_scalar(hi, hi, ROUND, None, ALU.add))
            link(nc.vector.tensor_scalar(hi, hi, ROUND, None, ALU.subtract))
            nc.vector.scalar_tensor_tensor(out=lo, in0=hi, scalar=-float(P), in1=pos, op0=ALU.mult, op1=ALU.add
                                           ).then_inc(places_done, 1)
            nc.vector.tensor_tensor(hot_hi[:, 2], view(tab, KNUM, [[0, PAIRS], [1, SLOTS]]),
                                    s_view(HI, [1, PAIRS], [0, SLOTS]), ALU.is_equal).then_inc(tiles_hot, 1)
            dve.wait_ge(tiles_hot, 1)
            nc.vector.tensor_scalar(hot_hi[:, 1], hot_hi[:, 2], tab[:, PLACE:PLACE + 1], None, ALU.mult).then_inc(hots_done, 1)
            dve.wait_ge(places_done, 1)
            for q in range(4):
                n = PAIRS // 4
                nc.vector.tensor_tensor(hot_lo[:, q * n:(q + 1) * n], view(tab, NUM, [[0, n], [1, P]]),
                                        s_view(LO + q * n, [1, n], [0, P]), ALU.is_equal).then_inc(hots_done, 1)
            dve.wait_ge(slots_done, 1)
            of_tile, in_tile, empty = ps[:, 4, 0:SLOTS], ps[:, 4, SLOTS:2 * SLOTS], s_view(EMPTY, [1, SLOTS])
            link(nc.vector.tensor_scalar(empty, in_tile, 0.0, tab[:, PAD:PAD + 1], ALU.is_equal, ALU.mult))
            link(nc.vector.tensor_tensor(empty, empty, of_tile, ALU.add))
            nc.vector.scalar_tensor_tensor(out=slot_x[:], in0=in_tile, scalar=-1.0, in1=empty, op0=ALU.add, op1=ALU.add
                                           ).then_inc(plan_done, 1)
            link(nc.vector.tensor_tensor(s_view(OWN, [E, SLOTS], [1, E]), view(tab, KNUM, [[1, SLOTS], [0, E]]),
                                         starts(1, 0, [0, SLOTS], [1, E]), ALU.is_ge))
            link(nc.vector.tensor_reduce(s_view(EXPERT, [1, SLOTS]), s_view(OWN, [E, SLOTS], [1, E]), AX, ALU.add))
            link(nc.vector.tensor_scalar(s_view(EXPERT, [1, SLOTS]), s_view(EXPERT, [1, SLOTS]), float(E - 1), None, ALU.min))
            nc.vector.tensor_copy(slot_e[:, 0:SLOTS], s_view(EXPERT, [1, SLOTS])).then_inc(experts_done, 1)
            link(nc.vector.tensor_tensor(s_view(OWN, [E, SLOTS], [1, E]), view(tab, NUM, [[0, SLOTS], [1, E]]),
                                         s_view(EXPERT, [1, SLOTS], [0, E]), ALU.is_equal))

            def slot_step(s, r, body):
                if body(s):
                    dve.wait_ge(xr_in[r], (s - r) * (16 // XR) + 16)
                    if not isinstance(s, int) or s >= 1:
                        dve.wait_ge(gate_done, s)
                    nc.vector.tensor_tensor(s_view(OWN_GATE, [1, E]), x_rows[:, r, C:C + E],
                                            view(scratch, s * E + OWN, [[1, E]]), ALU.mult).then_inc(gate_own, 1)
                    dve.wait_ge(gate_own, s + 1)
                    nc.vector.tensor_reduce(view(scratch, s + GATE, [[1, 1]]), s_view(OWN_GATE, [1, E]), AX, ALU.add
                                            ).then_inc(gate_done, 1)
                if body(s - 1):
                    dve.wait_ge(gelu_done, s)
                    if not isinstance(s, int) or s >= 3:
                        dve.wait_ge(gtr_done, s - 2)
                    nc.vector.tensor_tensor(gated[:, (r + 1) % 2], ps[:, (r + 1) % 2, C:2 * C], gelu1[:, (r + 1) % 2],
                                            ALU.mult).then_inc(gated_done, 1)
                if body(s - 3):
                    dve.wait_ge(ye_done, s - 2)
                    if not isinstance(s, int) or s >= 7:
                        dve.wait_ge(y_out, (s - 6) * 16)
                    nc.vector.tensor_scalar(y_rows[:, (r + 1) % 4], ps[:, 6 + (r + 1) % 2, 0:C],
                                            view(scratch, (s - 3) + GATE, [[1, 1]]), None, ALU.mult).then_inc(ye_out, 1)

            slot_steps(dve, slot_step)
            for c in range(NCH):
                for b in range(c * BPC, (c + 1) * BPC):
                    dve.wait_ge(ytr_done, b + 1)
                    xr = x_res[:, :, b * N:(b + 1) * N]
                    nc.vector.tensor_tensor(xr, xr, ps[:, b % 2, :].rearrange("p (h n) -> p h n", h=H), ALU.add
                                            ).then_inc(x4_done, 1)

        @block.tensor
        def _(pe):
            def group_norm(k, c):
                q = NCH * k + c
                pe.wait_ge(gn_sums[k], c + 1)
                if q >= 1:
                    pe.wait_ge(gn_var, q)
                for i in range(2):
                    last = nc.tensor.matmul(view(ps, GN_BANK[k] * CH, [[2, SPC], [1, 2]]), group_sb[:],
                                            stats[:, c, :, 3 * i:3 * i + 2], start=(i == 0), stop=(i == 1))
                last.then_inc(gn_group, 1)

            def normed(k, b):
                pe.wait_ge(xhat_act, B * k + b + 1)
                pe.wait_ge(xhat_dve, B * k + b + 1)

            pe.wait_ge(first_in, 16 * FIRST)
            def norms(c):
                pe.wait_ge(sq_done, c + 1)
                for h in range(H):
                    last = nc.tensor.matmul(bank(0), ones_sb[:], work[:, h * T + c * CH:h * T + (c + 1) * CH],
                                            start=(h == 0), stop=(h == H - 1))
                last.then_inc(n2_done, 1)

            def gram(c):
                pe.wait_ge(fn_done, c + 1)
                for t in range(TPC):
                    i, hb = c * TPC + t, t % 2
                    if i >= 2:
                        pe.wait_ge(gram_row, i - 1)
                    q0 = (i // 2) * N + (P - REACH if hb else 0)
                    for h in range(H):
                        last = nc.tensor.matmul(ps[:, 2 + i % 2, 0:ROW - REACH], work[:, h * T + i * P:h * T + (i + 1) * P],
                                                work[:, h * T + q0:h * T + q0 + ROW - REACH],
                                                start=(h == 0), stop=(h == H - 1))
                    last.then_inc(gram_done, 1)

            def conv_features(d, o):
                if d == 0:
                    pe.wait_ge(conv_in, 16 * CONV)
                if d >= 2:
                    pe.wait_ge(relu_done, H * (d - 2) + o + 1)
                for h in range(H):
                    nc.tensor.matmul(bank(CONV_BANK[d % 2][o]), conv_wT_sb[:, h, o * P:(o + 1) * P],
                                     x_hat[:, h, d * CH:(d + 1) * CH], start=(h == 0), stop=False)

            def turn_correlations(d):
                pe.wait_ge(cor_done, d + 1)
                pe.wait_ge(n2_floor, min(d + 2, NCH))
                for t in range(TPC):
                    last = nc.tensor.transpose(ps[0:NK, 0, t * P:(t + 1) * P],
                                               view(scratch, COR + (d * TPC + t) * NK, [[1, NK]]), ident[:])
                last.then_inc(cor_tr, 1)

            def conv_correlations(d):
                pe.wait_ge(cor_t_done, d + 1)
                for o in range(H):
                    nc.tensor.matmul(bank(CONV_BANK[d % 2][o]), conv_cT_sb[:, o * P:(o + 1) * P], cor_t[:, d * CH:(d + 1) * CH],
                                     start=False, stop=True).then_inc(y_done, 1)

            group_norm(0, 0)
            for t in range(NCH + 1):
                if t < NCH:
                    norms(t)
                if t + 1 < NCH:
                    group_norm(0, t + 1)
                if 0 <= t - 1:
                    conv_features(t - 1, 1)
                if t < NCH:
                    conv_features(t, 0)
                    gram(t)
                if 0 <= t - 1:
                    turn_correlations(t - 1)
                if 0 <= t - 2:
                    group_norm(1, t - 2)
                if 0 <= t - 1:
                    conv_correlations(t - 1)
            pe.wait_ge(relu_done, H * NCH)
            pe.wait_ge(consts_in, 16 * LATER)
            for n in range(2 * H * NCH):
                s, c = n // NCH, n % NCH
                h = s // 2
                if n == 1:
                    group_norm(1, NCH - 1)
                normed(1, BPC * (c + 1) - 1)
                if n >= 4:
                    pe.wait_ge(rest_done, n - 3)
                nc.tensor.matmul(bank(n % 4), qkv_sb[:, s % 2], x_hat[:, h, c * CH:(c + 1) * CH],
                                 start=True, stop=True).then_inc(qk_done, 1)
                normed(1, n // 2)
                if n >= 2:
                    pe.wait_ge(v_stored, n - 1)
                for h in range(H):
                    last = nc.tensor.matmul(ps[:, 6 + n % 2, h * P:(h + 1) * P], x_hat[:, h, n * P:(n + 1) * P],
                                            qkv_sb[:, 2], start=True, stop=True)
                last.then_inc(v_done, 1)

            def scores(U, u, g):
                i, mh, nh = u // 4, (u // 2) % 2, u % 2
                if u % 4 == 0:
                    pe.wait_ge(stack_in[i], (g + 1) * (2 * PARTS * 16))
                if later_than(U, 2):
                    pe.wait_ge(exp_done, U - 1)
                for b in (4, 5, 6, 7, 0, 1, 2, 3):
                    last = nc.tensor.matmul(ps[:, 2 * (u % 2) + b // 4, (b % 4) * P:(b % 4 + 1) * P],
                                            k_stack[:, i, b * N + mh * P:b * N + (mh + 1) * P],
                                            q_stack[:, i, b * N + nh * P:b * N + (nh + 1) * P],
                                            start=(b % 4 == 0), stop=(b % 4 == 3), skip_group_check=True)
                    if b == B - 1:
                        last.then_inc(scores_half, 1)
                last.then_inc(scores_done, 1)

            def subtract(U, u):
                pe.wait_ge(max_done, U + 1)
                for j in range(2):
                    last = nc.tensor.matmul(bank(2 * (u % 2) + j), ident_neg[:],
                                            view(m_bf, (u % 2) * P, [[0, B // 2], [1, P]]), start=False, stop=True,
                                            skip_group_check=True)
                last.then_inc(sub_done, 1)

            def total(U, u):
                pe.wait_ge(sum2_done, U + 1)
                if later_than(U, 2):
                    pe.wait_ge(ln_done, U - 1)
                for k in range(2):
                    last = nc.tensor.matmul(ps[:, 6 + u % 2, 0:P], ident[:], sum2[:, u % 2, k * P:(k + 1) * P],
                                            start=(k == 0), stop=(k == 1))
                last.then_inc(sum_done, 1)

            def product(U, u, g):
                i, mh, nh = u // 4, (u // 2) % 2, u % 2
                if u % 4 == 0:
                    pe.wait_ge(v_slot_ready[i], g + 1 if u < UPG - LAG else g)
                if u == 0 and later_than(U, 1):
                    pe.wait_ge(acc_out, g)
                pe.wait_ge(norm_pool, U + 1)
                pe.wait_ge(norm_dve, U + 1)
                for b in range(B):
                    last = nc.tensor.matmul(ps[32 * (b % 4):32 * (b % 4) + 32, 4, (b // 4) * N + nh * P:(b // 4) * N + (nh + 1) * P],
                                            v_slot[:, b * H + mh, i, :], e_ring[:, u % ER, b * P:(b + 1) * P],
                                            start=(u == 0 and b < 4), stop=(u == UPG - 1), skip_group_check=True)
                last.then_inc(pv_done, 1)

            def transpose_heads(group):
                pe.wait_ge(acc_out, group)
                for nh in range(H):
                    for j in range(2):
                        last = nc.tensor.transpose(ps[:, 5, (2 * nh + j) * P:(2 * nh + j + 1) * P],
                                                   o_sb[:, j * N + nh * P:j * N + (nh + 1) * P], ident[:])
                last.then_inc(acc_tr, 1)

            def attention_step(U, u, g, has):
                if has(0):
                    scores(U, u, g)
                if has(1):
                    subtract(U - 1, (u - 1) % UPG)
                if has(LAG):
                    product(U - LAG, (u - LAG) % UPG, g)
                if has(3):
                    total(U - 3, (u - 3) % UPG)
                if u == LAG + 1 and has(LAG + 2):
                    transpose_heads(g)

            pe.wait_ge(rest_done, 2 * H * NCH)
            attention_steps(pe, attention_step)
            transpose_heads(NG)

            group_norm(2, 0)
            group_norm(2, 1)

            def logits(c):
                normed(3, BPC * (c + 1) - 1)
                if c >= 1:
                    pe.wait_ge(logits_read, max(c - 1, 1))
                for t in range(c * TPC, (c + 1) * TPC):
                    for h in range(H):
                        last = nc.tensor.matmul(ps[:, 6, t * E:(t + 1) * E], x_hat[:, h, t * P:(t + 1) * P], gate_sb[:, h],
                                                start=(h == 0), stop=(h == H - 1))
                last.then_inc(logits_done, 1)

            def token_rows(b):
                normed(3, b)
                if b >= 1:
                    pe.wait_ge(row_done, b)
                for t in range(2):
                    for h in range(H):
                        last = nc.tensor.transpose(ps[:, 5, t * C + h * P:t * C + (h + 1) * P],
                                                   x_hat[:, h, (2 * b + t) * P:(2 * b + t + 1) * P], ident[:])
                last.then_inc(rtr_done, 1)

            def ranks(c):
                pe.wait_ge(mask_done, (1, 2, 2, 3)[c])
                if c == 0:
                    pe.wait_ge(gn_var, 4 * NCH)
                for t in range(c * TPC, (c + 1) * TPC):
                    nc.tensor.matmul(ps[:, 7, RANK + t * E:RANK + (t + 1) * E], before_bf[:], mask_bf[:, t],
                                     start=(t == 0), stop=True, skip_group_check=True)
                    last = nc.tensor.matmul(view(ps, 7 * CH + RANK + (t + 1) * E, [[E, TILES - t], [1, E]]), ones_bf[:],
                                            view(mask_bf, t * E, [[0, TILES - t], [1, E]]), start=False, stop=True,
                                            skip_group_check=True)
                last.then_inc(ranks_done, 1)

            for b in range(B + 1):
                if b < B:
                    normed(2, b)
                    if b >= 2:
                        pe.wait_ge(xt_done, b - 1)
                    for nh in range(2):
                        for h in range(H):
                            last = nc.tensor.transpose(ps[:, b % 2, nh * C + h * P:nh * C + (h + 1) * P],
                                                       x_hat[:, h, b * N + nh * P:b * N + (nh + 1) * P], ident[:])
                    last.then_inc(tr2_done, 1)
                    if b >= 1:
                        pe.wait_ge(cx_out, b)
                    for o in range(H):
                        for h in range(H):
                            last = nc.tensor.matmul(ps[:, 3, o * N:(o + 1) * N], gram_wT_sb[:, h, o * P:(o + 1) * P],
                                                    x_hat[:, h, b * N:(b + 1) * N], start=(h == 0), stop=(h == H - 1))
                    last.then_inc(cx_done, 1)
                if b >= 3 and b % 2 == 1:
                    group_norm(3, (b - 3) // 2)
                if b >= 1:
                    a = b - 1
                    pe.wait_ge(xx_out, a + 1)
                    pe.wait_ge(cx_out, a + 1)
                    if a >= 1:
                        pe.wait_ge(x3_done, a)
                    for o in range(H):
                        for h in range(H):
                            last = nc.tensor.matmul(ps[:, 4, o * N:(o + 1) * N], xxt[:, a % 2, h, o * P:(o + 1) * P],
                                                    cx[:, a % 2, h, :], start=(h == 0), stop=(h == H - 1))
                    last.then_inc(o_done, 1)
                if b < B:
                    pe.wait_ge(xt_done, b + 1)
                    if b >= 1:
                        pe.wait_ge(xx_out, b)
                    for o in range(H):
                        for n in range(2):
                            last = nc.tensor.matmul(ps[:, 2, o * C:(o + 1) * C], xt[:, b % 2, n, o * P:(o + 1) * P],
                                                    xt[:, b % 2, n, :], start=(n == 0), stop=(n == 1))
                    last.then_inc(xx_done, 1)

                if b == 1 or b == 2:
                    group_norm(2, b + 1)
                if b >= 4:
                    if b % 2 == 0:
                        logits((b - 4) // 2)
                    token_rows(b - 4)
            group_norm(3, NCH - 1)
            ranks(0)
            logits(NCH - 1)
            token_rows(B - 3)
            ranks(1)
            ranks(2)
            ranks(3)
            token_rows(B - 2)
            token_rows(B - 1)
            pe.wait_ge(tiles_scaled, 1)
            for q in range(4):
                pe.wait_ge(hots_done, q + 2)
                for j in range(q * PAIRS // 4, (q + 1) * PAIRS // 4):
                    last = nc.tensor.matmul(ps[:, 4, 0:2 * SLOTS], hot_lo[:, j], hot_hi[:, 0:2, j],
                                            start=(j == 0), stop=(j == PAIRS - 1))
            last.then_inc(slots_done, 1)
            pe.wait_ge(w_in, 64)
            pe.wait_ge(experts_done, 1)

            def slot_step(s, r, body):
                if body(s):
                    pe.wait_ge(xr_in[r], (s - r) * (16 // XR) + 16)
                    if not isinstance(s, int) or s >= 2:
                        pe.wait_ge(xt_out, s - 1)
                    for h in range(H):
                        last = nc.tensor.transpose(ps[:, 2 + r % 2, h * P:(h + 1) * P], x_rows[:, r, h * P:(h + 1) * P], ident[:])
                    last.then_inc(xtr_done, 1)
                if body(s - 1):
                    e = pe.value_load(slot_e[0:1, bass.ds(s - 1, 1)], min_val=0, max_val=E - 1)
                    pe.wait_ge(xt_out, s)
                    if not isinstance(s, int) or s >= 3:
                        pe.wait_ge(gated_done, s - 2)
                    for h in range(H):
                        last = nc.tensor.matmul(bank((r + 1) % 2), x_turned[:, (r + 1) % 2, h * P:(h + 1) * P],
                                                w13_sb[:, h, bass.ds(e * (2 * C), 2 * C)], start=(h == 0), stop=(h == H - 1))
                    last.then_inc(h_done, 1)
                if body(s - 2):
                    pe.wait_ge(gated_done, s - 1)
                    if not isinstance(s, int) or s >= 4:
                        pe.wait_ge(gt_done, s - 3)
                    for f in range(2):
                        last = nc.tensor.transpose(ps[:, 4 + r % 2, f * P:(f + 1) * P], gated[:, r % 2, f * P:(f + 1) * P], ident[:])
                    last.then_inc(gtr_done, 1)
                if body(s - 3):
                    e = pe.value_load(slot_e[0:1, bass.ds(s - 3, 1)], min_val=0, max_val=E - 1)
                    pe.wait_ge(gt_done, s - 2)
                    if not isinstance(s, int) or s >= 5:
                        pe.wait_ge(ye_out, s - 4)
                    for f in range(2):
                        last = nc.tensor.matmul(ps[:, 6 + (r + 1) % 2, 0:C], gated_t[:, (r + 1) % 2, f * P:(f + 1) * P],
                                                w2_sb[:, f, bass.ds(e * C, C)], start=(f == 0), stop=(f == 1))
                    last.then_inc(ye_done, 1)

            slot_steps(pe, slot_step)
            for b in range(B):
                pe.wait_ge(y_in[b], 16)
                if b >= 2:
                    pe.wait_ge(x4_done, b - 1)
                for h in range(H):
                    for nh in range(2):
                        last = nc.tensor.transpose(ps[:, b % 2, h * N + nh * P:h * N + (nh + 1) * P],
                                                   y_back[:, 2 * b + nh, h * P:(h + 1) * P], ident[:])
                last.then_inc(ytr_done, 1)


def _arrays(x, L0_conv_conv_w, L0_conv_conv_b, L1_conv_w_qkv, L1_conv_b_qkv, L2_conv_W, L2_conv_gamma,
            L3_conv_gate_w, L3_conv_w1, L3_conv_w2, L3_conv_w3):
    import numpy as np
    f = np.float32
    C, P, D, S, K = 256, 128, 8, 16, 5
    E = L3_conv_w1.shape[0]
    conv_w = np.asarray(L0_conv_conv_w)
    w_qkv, b_qkv = np.asarray(L1_conv_w_qkv), np.asarray(L1_conv_b_qkv)
    blocks = np.zeros((3, P, P), f)
    for s in range(3):
        for r in range(P // D):
            blocks[s, r * D:(r + 1) * D, r * D:(r + 1) * D] = w_qkv[s * D:(s + 1) * D].T
    w13T = np.stack([np.asarray(L3_conv_w1), np.asarray(L3_conv_w3)], 1)
    col = np.arange(P) % S
    shift = np.arange(K) - K // 2
    inside = (col[:, None] + shift[None] >= 0) & (col[:, None] + shift[None] < S)
    group = np.arange(P) // 8
    TILES, T = 16, 2048
    SLOTS = (2 * T + E * (P - 1)) // P
    place = np.arange(P)[:, None]
    tables = np.concatenate([np.broadcast_to(np.arange(P), (P, P)), np.broadcast_to(np.arange(SLOTS), (P, SLOTS)),
                             np.broadcast_to(np.tile(np.arange(TILES) * P, 2), (P, 2 * TILES)), place + 1, T + 1 + place], 1)
    return {
        "x": np.asarray(x),
        "conv_wT": conv_w[:, :C].T.reshape(2, P, C),
        "conv_cT": conv_w[:, C:].T,
        "conv_b": np.asarray(L0_conv_conv_b).reshape(2, P).T,
        "qkv_blocks": blocks,
        "qk_bias": np.stack([np.tile(b_qkv[:D], P // D), np.tile(b_qkv[D:2 * D], P // D)], 1),
        "v_bias": np.broadcast_to(b_qkv[2 * D:], (P, D)),
        "gram_wT": np.asarray(L2_conv_W).T.reshape(2, P, C),
        "gamma": np.broadcast_to(np.asarray(L2_conv_gamma).reshape(1, 1), (P, 1)),
        "gate_wT": np.asarray(L3_conv_gate_w).T,
        "w13T": w13T.transpose(3, 0, 1, 2).reshape(2, P, E * 2 * C),
        "w2T": np.asarray(L3_conv_w2).transpose(2, 0, 1).reshape(2, P, E * C),
        "identity": np.eye(P, dtype=f),
        "ones": np.ones((P, P), f),
        "group_ones": (group[:, None] == group[None]).astype(f) / f(16),
        "edge_mask": inside.astype(f),
        "expert_rank": np.broadcast_to(np.arange(E, 0, -1).astype(f), (P, E)),
        "before": (np.arange(P)[:, None] < np.arange(P)[None]).astype(f),
        "tables": tables.astype(f),
    }


def kernel(**inputs):
    import numpy as _np
    import concourse.bacc as _bacc
    from concourse import mybir as _mybir
    from concourse.bass_utils import run_bass_kernel_spmd as _run

    nc = _bacc.Bacc("TRN2", target_bir_lowering=False, num_devices=1)
    arrays, args = {}, []
    for name, a in _arrays(**inputs).items():
        a = _np.ascontiguousarray(a)
        arrays[f"in_{name}_dram"] = a
        args.append(nc.dram_tensor(f"in_{name}_dram", a.shape, _mybir.dt.from_np(a.dtype), kind="ExternalInput").ap())
    shape = tuple(inputs["x"].shape)
    args.append(nc.dram_tensor("out_0_dram", shape, _mybir.dt.float32, kind="ExternalOutput").ap())
    conv_stack_kernel(nc, *args)
    r = _run(nc, [arrays], core_ids=[0])
    return r.results[0]["out_0_dram"]
```
